# Optimizing a Trainium2 kernel written in Bass

```python
import numpy as np
import jax
import jax.numpy as jnp

def _softmax(x, axis=-1):
    return jax.nn.softmax(x, axis=axis)

def _gelu(x):
    return jax.nn.gelu(x, approximate=True)

def _silu(x):
    return jax.nn.silu(x)

def _sigmoid(x):
    return jax.nn.sigmoid(x)

def _layernorm(x, axis=-1, eps=1e-05):
    m = jnp.mean(x, axis=axis, keepdims=True)
    v = jnp.var(x, axis=axis, keepdims=True)
    return (x - m) / jnp.sqrt(v + eps)

def _scatter_add(tgt, idx, src, axis=0):
    return tgt.at[idx].add(src)

def _segment_sum(src, seg, n):
    return jax.ops.segment_sum(src, seg, n)
kernel_name = 'mk_flamingo_gated_d1_seqx_r4_14b053'

def setup_inputs(seed: int=0):
    np.random.seed(seed)
    _w = jnp.asarray

    def _rec_inputs():
        import jax
        import jax.numpy as jnp
        _rk = jax.random.key(seed)
        x = 7.22e-05 + 1 * jax.random.normal(jax.random.fold_in(_rk, 1), (32, 100, 256), jnp.float32)
        _lenS = 100 - jax.random.randint(jax.random.fold_in(_rk, 7), (32,), 0, max(1, 100 // 4) + 1, jnp.int32)
        _lenS2 = 361 - jax.random.randint(jax.random.fold_in(_rk, 8), (32,), 0, max(1, 361 // 4) + 1, jnp.int32)
        _ctx_1024P = jax.random.normal(jax.random.fold_in(_rk, 11), (32, 16, 256), jnp.float32)
        _ctx_1024c = jax.random.dirichlet(jax.random.fold_in(_rk, 511), 0.3 * jnp.ones((16,), jnp.float32), (32, 361))
        _ctx_1024t = jnp.einsum('bsk,bkd->bsd', _ctx_1024c, _ctx_1024P)
        _ctx_1024t = _ctx_1024t * jax.lax.rsqrt(jnp.mean(jnp.square(_ctx_1024t)) + 1e-12) * 0.953939
        ctx_1024 = 4.13588e-05 + 0.999923 * (_ctx_1024t + 0.3 * jax.random.normal(jax.random.fold_in(_rk, 611), (32, 361, 256), jnp.float32))
        _g = jax.random.normal(jax.random.fold_in(_rk, 9001), (2, 1), jnp.float32)
        _g = jnp.sign(_g) * jnp.maximum(jnp.abs(_g), 1.0) + (_g == 0) * 1.0
        g_xattn = _g[0]
        g_ffn = _g[1]
        return (x, ctx_1024, g_xattn, g_ffn)
    x, ctx_1024, g_xattn, g_ffn = _rec_inputs()

    def _L0_xattn_setup():
        import jax, jax.numpy as jnp
        import numpy as np
        EMBED_DIM = 256
        HEADS = 16
        HEAD_DIM = EMBED_DIM // HEADS
        key = jax.random.key(seed)
        ks = jax.random.split(key, 12)
        B, Sq, Sk, E = (4, 512, 512, EMBED_DIM)
        s = 1.0 / np.sqrt(E)
        return {'query': jax.random.normal(ks[0], (B, Sq, E), jnp.float32), 'key': jax.random.normal(ks[1], (B, Sk, E), jnp.float32), 'value': jax.random.normal(ks[2], (B, Sk, E), jnp.float32), 'Wq': jax.random.normal(ks[3], (E, E), jnp.float32) * s, 'bq': jnp.zeros((E,), jnp.float32), 'Wk': jax.random.normal(ks[4], (E, E), jnp.float32) * s, 'bk': jnp.zeros((E,), jnp.float32), 'Wv': jax.random.normal(ks[5], (E, E), jnp.float32) * s, 'bv': jnp.zeros((E,), jnp.float32), 'Wo': jax.random.normal(ks[6], (E, E), jnp.float32) * s, 'bo': jnp.zeros((E,), jnp.float32)}
    _L0_xattn_all = _L0_xattn_setup()
    _L0_xattn_in = {k: v for k, v in _L0_xattn_all.items() if k in ('Wq', 'bq', 'Wk', 'bk', 'Wv', 'bv', 'Wo', 'bo')}
    del _L0_xattn_all

    def _L0_ffn_setup():
        import jax, jax.numpy as jnp
        import numpy as np
        B, S, H = (2, 256, 256)
        E, I, SI = (8, 128, 512)
        TOP_K, N_GROUP, TOPK_GROUP = (2, 2, 1)
        ROUTED_SCALE = 2.5

        def _route(x2d, gate_weight, gate_bias):
            T = x2d.shape[0]
            logits = x2d @ gate_weight.T
            scores = jax.nn.sigmoid(logits)
            sfc = scores + gate_bias[None, :]
            g = sfc.reshape(T, N_GROUP, E // N_GROUP)
            group_scores = jax.lax.top_k(g, 2)[0].sum(-1)
            _, gidx = jax.lax.top_k(group_scores, TOPK_GROUP)
            gmask = jnp.zeros((T, N_GROUP), sfc.dtype).at[jnp.arange(T)[:, None], gidx].set(1.0)
            smask = jnp.repeat(gmask, E // N_GROUP, axis=1)
            masked = jnp.where(smask > 0, sfc, 0.0)
            _, topk_idx = jax.lax.top_k(masked, TOP_K)
            topk_w = jnp.take_along_axis(scores, topk_idx, axis=1)
            topk_w = topk_w / (topk_w.sum(-1, keepdims=True) + 1e-20)
            topk_w = topk_w * ROUTED_SCALE
            return (topk_idx, topk_w)
        key = jax.random.key(seed)
        ks = jax.random.split(key, 7)

        def w(k, shape, sc=0.02):
            return jax.random.normal(k, shape, jnp.float32) * sc
        return {'hidden_states': jax.random.normal(ks[0], (B, S, H), jnp.float32), 'gate_weight': w(ks[1], (E, H)), 'gate_bias': w(ks[2], (E,), 0.01), 'up_weights': w(ks[3], (E, I, H)), 'down_weights': w(ks[4], (E, H, I)), 'shared_up_weight': w(ks[5], (SI, H)), 'shared_down_weight': w(ks[6], (H, SI))}
    _L0_ffn_all = _L0_ffn_setup()
    _L0_ffn_in = {k: v for k, v in _L0_ffn_all.items() if k in ('gate_weight', 'gate_bias', 'up_weights', 'down_weights', 'shared_up_weight', 'shared_down_weight')}
    del _L0_ffn_all
    return {'x': x, 'ctx_1024': ctx_1024, 'g_xattn': g_xattn, 'g_ffn': g_ffn, 'L0_xattn_Wq': _L0_xattn_in['Wq'], 'L0_xattn_bq': _L0_xattn_in['bq'], 'L0_xattn_Wk': _L0_xattn_in['Wk'], 'L0_xattn_bk': _L0_xattn_in['bk'], 'L0_xattn_Wv': _L0_xattn_in['Wv'], 'L0_xattn_bv': _L0_xattn_in['bv'], 'L0_xattn_Wo': _L0_xattn_in['Wo'], 'L0_xattn_bo': _L0_xattn_in['bo'], 'L0_ffn_gate_weight': _L0_ffn_in['gate_weight'], 'L0_ffn_gate_bias': _L0_ffn_in['gate_bias'], 'L0_ffn_up_weights': _L0_ffn_in['up_weights'], 'L0_ffn_down_weights': _L0_ffn_in['down_weights'], 'L0_ffn_shared_up_weight': _L0_ffn_in['shared_up_weight'], 'L0_ffn_shared_down_weight': _L0_ffn_in['shared_down_weight']}

def reference(x, ctx_1024, g_xattn, g_ffn, L0_xattn_Wq, L0_xattn_bq, L0_xattn_Wk, L0_xattn_bk, L0_xattn_Wv, L0_xattn_bv, L0_xattn_Wo, L0_xattn_bo, L0_ffn_gate_weight, L0_ffn_gate_bias, L0_ffn_up_weights, L0_ffn_down_weights, L0_ffn_shared_up_weight, L0_ffn_shared_down_weight):
    import jax
    import jax.numpy as jnp

    def _L0_xattn_ref(query, key, value, Wq, bq, Wk, bk, Wv, bv, Wo, bo):
        import jax, jax.numpy as jnp
        import numpy as np
        EMBED_DIM = 256
        HEADS = 16
        HEAD_DIM = EMBED_DIM // HEADS
        B, Sq, E = query.shape
        Sk = key.shape[1]
        H, D = (HEADS, HEAD_DIM)
        Q = (query @ Wq + bq).reshape(B, Sq, H, D).transpose(0, 2, 1, 3)
        K = (key @ Wk + bk).reshape(B, Sk, H, D).transpose(0, 2, 1, 3)
        V = (value @ Wv + bv).reshape(B, Sk, H, D).transpose(0, 2, 1, 3)
        scores = jnp.einsum('bhqd,bhkd->bhqk', Q, K) / jnp.sqrt(jnp.float32(D))
        attn = jax.nn.softmax(scores, axis=-1)
        out = jnp.einsum('bhqk,bhkd->bhqd', attn, V)
        out = out.transpose(0, 2, 1, 3).reshape(B, Sq, E)
        return out @ Wo + bo

    def _L0_ffn_ref(hidden_states, gate_weight, gate_bias, up_weights, down_weights, shared_up_weight, shared_down_weight):
        import jax, jax.numpy as jnp
        import numpy as np
        B, S, H = (2, 256, 256)
        E, I, SI = (8, 128, 512)
        TOP_K, N_GROUP, TOPK_GROUP = (2, 2, 1)
        ROUTED_SCALE = 2.5

        def _route(x2d, gate_weight, gate_bias):
            T = x2d.shape[0]
            logits = x2d @ gate_weight.T
            scores = jax.nn.sigmoid(logits)
            sfc = scores + gate_bias[None, :]
            g = sfc.reshape(T, N_GROUP, E // N_GROUP)
            group_scores = jax.lax.top_k(g, 2)[0].sum(-1)
            _, gidx = jax.lax.top_k(group_scores, TOPK_GROUP)
            gmask = jnp.zeros((T, N_GROUP), sfc.dtype).at[jnp.arange(T)[:, None], gidx].set(1.0)
            smask = jnp.repeat(gmask, E // N_GROUP, axis=1)
            masked = jnp.where(smask > 0, sfc, 0.0)
            _, topk_idx = jax.lax.top_k(masked, TOP_K)
            topk_w = jnp.take_along_axis(scores, topk_idx, axis=1)
            topk_w = topk_w / (topk_w.sum(-1, keepdims=True) + 1e-20)
            topk_w = topk_w * ROUTED_SCALE
            return (topk_idx, topk_w)
        Bv, Sv, Hv = hidden_states.shape
        x = hidden_states.reshape(-1, Hv)
        T = x.shape[0]
        topk_idx, topk_w = _route(x, gate_weight, gate_bias)
        cw = jnp.zeros((T, E), x.dtype).at[jnp.arange(T)[:, None], topk_idx].add(topk_w)
        h = jnp.einsum('th,eih->tei', x, up_weights)
        r = jnp.maximum(h, 0.0)
        r2 = r * r
        routed = jnp.einsum('tei,ehi,te->th', r2, down_weights, cw)
        sh = jnp.maximum(x @ shared_up_weight.T, 0.0)
        shared = sh * sh @ shared_down_weight.T
        return (routed + shared).reshape(Bv, Sv, Hv)
    x = x + jnp.tanh(g_xattn[0]) * _L0_xattn_ref(_layernorm(x, axis=-1), ctx_1024, ctx_1024, L0_xattn_Wq, L0_xattn_bq, L0_xattn_Wk, L0_xattn_bk, L0_xattn_Wv, L0_xattn_bv, L0_xattn_Wo, L0_xattn_bo)
    x = x + jnp.tanh(g_ffn[0]) * _L0_ffn_ref(_layernorm(x, axis=-1), L0_ffn_gate_weight, L0_ffn_gate_bias, L0_ffn_up_weights, L0_ffn_down_weights, L0_ffn_shared_up_weight, L0_ffn_shared_down_weight)
    return x

_drawn_inputs = setup_inputs


def setup_inputs(seed=0):
    import zlib

    import numpy as np

    out = dict(_drawn_inputs(seed))
    spreads = {'L0_xattn_bq': (0.0, 0.464),
     'L0_xattn_bk': (0.0, 0.8),
     'L0_xattn_bv': (0.0, 0.1),
     'L0_xattn_bo': (0.0, 0.1)}
    factors = {'L0_ffn_gate_bias': 4.445}
    for name, (base, spread) in spreads.items():
        noise = np.random.default_rng([zlib.crc32(name.encode()), seed]).standard_normal(out[name].shape)
        drawn = base * np.exp(spread * noise) if base else spread * noise
        out[name] = jnp.asarray(drawn.astype(out[name].dtype))
    for name, factor in factors.items():
        out[name] = (out[name] * factor).astype(out[name].dtype)
    return out
```

```python
from contextlib import ExitStack

import concourse.bass as bass
from concourse import mybir

F32 = mybir.dt.float32
BF16 = mybir.dt.bfloat16
ALU = mybir.AluOpType
ACT = mybir.ActivationFunctionType
AX_X = mybir.AxisListType.X

B, SQ, SK, E = 32, 100, 361, 256
H, D = 16, 16
CI = E // 128
TOK = B * SQ
NE, HID, SHARED = 8, 128, 512
NJ = NE + SHARED // HID
EPS = 1e-5
SCALE = float(D) ** -0.5
ROUTED_SCALE = 2.5
K_PARTS = (0, 1, 2, 0, 1, 0)
Q_PARTS = (0, 0, 0, 1, 1, 2)
ROWS = 6 * D
MROWS = ROWS + 2
KT = 121
KSTEP = 120
NT = 3
PIECES = H * NT
PER_UNIT = 5
UNITS = -(-PIECES // PER_UNIT)
DV = D + 1
QG = 4
GT = 4
TILES = TOK // 128
GROUPS = -(-TILES // GT)
ROUTER_OPS = 19


def unit_pieces(u):
    js = range(u * PER_UNIT, min((u + 1) * PER_UNIT, PIECES))
    return [(j // NT, j % NT, (j % PER_UNIT) * SQ) for j in js]


def wait(eng, sem, value):
    if not (isinstance(value, int) and value <= 0):
        eng.wait_ge(sem, value)


class At:

    def __init__(self, k, c):
        self.k, self.c = k, c
        self.buf = c % 3
        self.round = k + c // 3
        self.n = k * 3 + c

    def __add__(self, d):
        return At(self.k, self.c + d)


def build(nc, x, ctx_t, g_x, g_f, wq, bq, wk, bk, wv, bv, wo, bo, gate_t, gate_b, up_t, down_t, sup_t, sdown_t, out):
    kscr = nc.dram_tensor("kscr", [B, 3, E, SK], BF16, kind="Internal").ap()
    qscr = nc.dram_tensor("qscr", [B, 3, E, SQ], BF16, kind="Internal").ap()
    x2scr = nc.dram_tensor("x2scr", [TOK, E], F32, kind="Internal").ap()

    with ExitStack() as ctx:
        def sb(name, shape, dt=F32):
            return ctx.enter_context(nc.sbuf_tensor(name, shape, dt))

        def sem(name):
            return ctx.enter_context(nc.semaphore(name))

        psum = ctx.enter_context(nc.psum_tensor("psum", [128, 8, 512], F32))

        ident = sb("ident", [128, 128])
        wq_s, wk_s, wv_s, wo_s = (sb(n, [128, CI, E]) for n in ("wq_s", "wk_s", "wv_s", "wo_s"))
        bq_s, bk_s = sb("bq_s", [128, 2]), sb("bk_s", [128, 2])
        bv_s, bo_s, gbo = sb("bv_s", [SQ, E]), sb("bo_s", [SQ, E]), sb("gbo", [SQ, E])
        up_s = sb("up_s", [128, CI, NJ * HID])
        down_s = sb("down_s", [128, NJ, E])
        gate_s = sb("gate_s", [128, CI, NE])
        gb_s = sb("gb_s", [128, NE])
        lower = sb("lower", [128, NE, NE])
        g_raw, g_tanh = sb("g_raw", [128, 2]), sb("g_tanh", [128, 2])
        half_neg = sb("half_neg", [128, GT])
        eps_s, zero = sb("eps_s", [128, GT]), sb("zero", [128, 1])

        xin = sb("xin", [128, 2, GT, E])
        xn = sb("xn", [128, 2, GT, E])
        xnt = sb("xnt", [128, 2, CI, GT * 128])
        stats = sb("stats", [128, 2, GT, 6])
        carrier = sb("carrier", [128, 1])
        meanvar = sb("meanvar", [128, 2, GT, 2])
        vareps = sb("vareps", [128, 2, GT])
        rstd = sb("rstd", [128, 2, GT])

        qf = sb("qf", [128, 2, QG * SQ])
        qr = sb("qr", [128, 2, QG * SQ])
        qp = sb("qp", [128, 2, 3, 2, QG * SQ], BF16)

        ctxt = sb("ctxt", [128, 3, CI, SK])
        kf = sb("kf", [128, 2, SK])
        kr = sb("kr", [128, 2, SK])
        kp = sb("kp", [128, 3, 3, 2, SK], BF16)
        ks = sb("ks", [128, 3, H, SK], BF16)
        qs = sb("qs", [128, 3, H, SQ], BF16)
        vs = sb("vs", [128, 3, NT, H, DV])
        negmax = sb("negmax", [SQ, H])
        mrow = sb("mrow", [H, 2, SQ], BF16)
        probs = sb("probs", [128, UNITS, PER_UNIT * SQ])
        rden = sb("rden", [SQ, H])
        att0, att = sb("att0", [SQ, E]), sb("att", [SQ, E])
        att_t = sb("att_t", [128, CI, SQ])
        xr = sb("xr", [SQ, 3, E])
        xb = sb("xb", [SQ, 3, E])
        x2 = sb("x2", [SQ, 3, E])

        relu = sb("relu", [128, 2, GT * 128])
        gated = sb("gated", [128, 2, GT * 128])
        sq = sb("sq", [128, 2, GT * 128])
        cw = sb("cw", [128, 2, GT, NE])
        rt = sb("rt", [128, 12, GT, NE])
        big = sb("big", [128, 2, GT, NE, NE])
        y = probs[:].rearrange("p u n -> p (u n)")[:, 0:2 * GT * E].rearrange("p (a t e) -> p a t e", a=2, t=GT)

        consts = sem("consts")
        made = sem("made")
        fills = sem("fills")
        gates_ready = sem("gates_ready")
        gbo_ready = sem("gbo_ready")
        xin_in = [sem(f"xin_in{i}") for i in range(2)]
        stats_done, meanvar_ready, vareps_ready = sem("stats_done"), sem("meanvar_ready"), sem("vareps_ready")
        rstd_ready, xn_ready = sem("rstd_ready"), sem("xn_ready")
        xnt_mm, xnt_ready = sem("xnt_mm"), sem("xnt_ready")
        q_mm, qf_ready, q_chain, qp_ready = sem("q_mm"), sem("qf_ready"), sem("q_chain"), sem("qp_ready")
        qscr_out = [sem(f"qscr_out{i}") for i in range(2)]

        ctx_in = [sem(f"ctx_in{i}") for i in range(3)]
        xr_in = [sem(f"xr_in{i}") for i in range(3)]
        qs_in = [sem(f"qs_in{i}") for i in range(3)]
        ks_in = [sem(f"ks_in{i}") for i in range(3)]
        m_in = [sem(f"m_in{i}") for i in range(3)]
        kscr_out = [sem(f"kscr_out{i}") for i in range(3)]
        x2_out = [sem(f"x2_out{i}") for i in range(3)]
        k_mm, k_ready, k_chain, kp_ready = sem("k_mm"), sem("k_ready"), sem("k_chain"), sem("kp_ready")
        v_mm, v_ready = sem("v_mm"), sem("v_ready")
        row_mm, max_ready, mt_mm, mhi_ready, mrow_ready = (
            sem("row_mm"), sem("max_ready"), sem("mt_mm"), sem("mhi_ready"), sem("mrow_ready"))
        score_mm, exp_ready, pv_mm = sem("score_mm"), sem("exp_ready"), sem("pv_mm")
        rden_ready, att0_ready, att_ready = sem("rden_ready"), sem("att0_ready"), sem("att_ready")
        att_t_mm, att_t_ready, o_mm, xb_ready, x2_ready = (
            sem("att_t_mm"), sem("att_t_ready"), sem("o_mm"), sem("xb_ready"), sem("x2_ready"))

        ln_in = [sem(f"ln_in{i}") for i in range(2)]
        t_stats, t_meanvar, t_vareps, t_rstd, t_xn = (
            sem("t_stats"), sem("t_meanvar"), sem("t_vareps"), sem("t_rstd"), sem("t_xn"))
        t_xnt_mm, t_xnt = sem("t_xnt_mm"), sem("t_xnt")
        logit_mm, esig_ready, router, cw_ready = sem("logit_mm"), sem("esig_ready"), sem("router"), sem("cw_ready")
        up_mm, relu_ready, cwb_mm, gated_ready, sq_ready, down_mm = (
            sem("up_mm"), sem("relu_ready"), sem("cwb_mm"), sem("gated_ready"), sem("sq_ready"), sem("down_mm"))
        norm_chain = sem("norm_chain")
        y_ready = sem("y_ready")
        y_out = [sem(f"y_out{i}") for i in range(2)]

        N_CONST = 18 * 16

        ROW_BANK, SCORE_BANK, PV_BANK, D0, D1, D2 = (0, 1), (2, 3), 4, 5, 6, 7
        UP_BANK, CWB_BANK, DOWN_BANK, LN_BANK, LOGIT_BANK = (0, 1), (2, 3), 4, 6, 7

        def loop_groups0(eng, do):
            for g in range(2):
                do(g, g, 0)
            with eng.Fori(1, B // QG // 2) as k:
                for p in range(2):
                    do(k * 2 + p, p, k)

        def phase1(eng, do):
            def full(k, c):
                do(At(k, c + 2), At(k, c + 1), At(k, c), At(k, c - 1))

            def edge(s):
                at = [At((s + d) // 3, (s + d) % 3) if 0 <= s + d < B else None for d in (2, 1, 0, -1)]
                do(*at)

            for s in range(-2, 3):
                edge(s)
            with eng.Fori(1, (B - 2) // 3) as k:
                for c in range(3):
                    full(k, c)
            for s in range(B - 2, B + 1):
                edge(s)

        def tiles_of(g):
            return min(GT, TILES - g * GT) if isinstance(g, int) else GT

        def phase2(eng, ln, ffn):
            def whole(g, p, k):
                for part in ("norm", 0, 1, 2, 3, "route"):
                    ln(g, p, k, part)

            def ahead(g, p, k):
                return lambda part: ln(g, p, k, part)

            whole(0, 0, 0)
            ffn(0, 0, 0, ahead(1, 1, 0))
            with eng.Fori(0, 2) as k:
                ffn(k * 2 + 1, 1, k, ahead(k * 2 + 2, 0, k + 1))
                ffn(k * 2 + 2, 0, k + 1, ahead(k * 2 + 3, 1, k + 1))
            ffn(5, 1, 2, ahead(6, 0, 3))
            ffn(6, 0, 3, lambda part: None)

        block = ctx.enter_context(nc.Block())

        @block.sync
        def _(sp):
            for dst, src in (
                (wq_s, wq.rearrange("(c p) n -> p c n", p=128)), (wk_s, wk.rearrange("(c p) n -> p c n", p=128)),
                (wv_s, wv.rearrange("(c p) n -> p c n", p=128)), (wo_s, wo.rearrange("(c p) n -> p c n", p=128)),
                (bv_s, bv.partition_broadcast(SQ)), (bo_s, bo.partition_broadcast(SQ)),
                (gb_s, gate_b.partition_broadcast(128)),
                (gate_s, gate_t.rearrange("(c p) n -> p c n", p=128)),
            ):
                sp.dma_start(dst[:], src).then_inc(consts, 16)
            for half in range(2):
                sp.dma_start(bq_s[:, half:half + 1], bq.rearrange("(a p o) -> a p o", p=128, o=1)[half]).then_inc(consts, 16)
                sp.dma_start(bk_s[:, half:half + 1], bk.rearrange("(a p o) -> a p o", p=128, o=1)[half]).then_inc(consts, 16)
            for n, g in enumerate((g_x, g_f)):
                sp.dma_start(g_raw[:, n:n + 1], g.partition_broadcast(128)).then_inc(consts, 16)
            sp.dma_start(up_s[:, :, 0:SHARED], sup_t.rearrange("(c p) n -> p c n", p=128)).then_inc(consts, 16)
            sp.dma_start(up_s[:, :, SHARED:], up_t.rearrange("(c p) n -> p c n", p=128)).then_inc(consts, 16)
            sp.dma_start(down_s[:, 0:SHARED // HID, :], sdown_t.rearrange("(j p) n -> p j n", p=HID)).then_inc(consts, 16)
            sp.dma_start(down_s[:, SHARED // HID:, :], down_t.rearrange("(j p) n -> p j n", p=HID)).then_inc(consts, 16)

            x_v = x.rearrange("(g b q) e -> g q b e", b=QG, q=SQ)

            def load_x(g, p, k):
                wait(sp, xn_ready, (g - 1) * QG)
                sp.dma_start(xin[0:SQ, p], x_v[g]).then_inc(xin_in[p], 16)

            def group0(g, p, k):
                if not (isinstance(g, int) and g < 2):
                    load_x(g, p, k)
                sp.wait_ge(qp_ready, g + 1)
                for i in range(QG):
                    sp.dma_start(qscr[g * QG + i].rearrange("r (a p) q -> p r a q", p=128),
                                 qp[:, p, :, :, i * SQ:(i + 1) * SQ]).then_inc(qscr_out[p], 16)

            load_x(0, 0, 0)
            load_x(1, 1, 0)
            loop_groups0(sp, group0)
            for p in range(2):
                sp.wait_ge(qscr_out[p], QG * 16 * (B // QG // 2))

            def load_ctx(b):
                wait(sp, v_mm, NT * (b.n - 2))
                sp.dma_start(ctxt[:, b.buf], ctx_t[b.n].rearrange("(c p) n -> p c n", p=128)).then_inc(ctx_in[b.buf], 16)

            def step(bp, bm, be, bf):
                if bp is not None:
                    load_ctx(bp)
                    wait(sp, score_mm, UNITS * (bp.n - 2))
                    for r in range(6):
                        sp.dma_start(qs[r * D:(r + 1) * D, bp.buf],
                                     qscr[bp.n, Q_PARTS[r]].rearrange("(d h) q -> d h q", h=H)).then_inc(qs_in[bp.buf], 16)
                if bm is not None:
                    wait(sp, xb_ready, bm.n - 2)
                    sp.dma_start(xr[:, bm.buf], x[bass.ds(bm.n * SQ, SQ), :]).then_inc(xr_in[bm.buf], 16)
                if bp is not None:
                    sp.wait_ge(kp_ready, bp.n + 1)
                    sp.dma_start(kscr[bp.n].rearrange("r (a p) k -> p r a k", p=128), kp[:, bp.buf]).then_inc(kscr_out[bp.buf], 16)
                    sp.wait_ge(kscr_out[bp.buf], (bp.round + 1) * 16)
                    kv = kscr[bp.n].rearrange("r (d h) k -> (r d) (h k)", h=H)
                    for lo, n in ((0, 3), (3, 2), (5, 1)):
                        sp.dma_start(ks[lo * D:(lo + n) * D, bp.buf], kv[0:n * D].rearrange("p (h k) -> p h k", h=H)).then_inc(ks_in[bp.buf], 16)
                if bf is not None:
                    sp.wait_ge(x2_ready, bf.n + 1)
                    sp.dma_start(x2scr[bass.ds(bf.n * SQ, SQ), :], x2[:, bf.buf]).then_inc(x2_out[bf.buf], 16)
                if bm is not None:
                    sp.wait_ge(mrow_ready, bm.n + 1)
                    for r in range(2):
                        sp.dma_start(qs[ROWS + r:ROWS + r + 1, bm.buf], mrow[:, r, :]).then_inc(m_in[bm.buf], 16)

            phase1(sp, step)
            for i in range(3):
                sp.wait_ge(x2_out[i], 16 * len(range(i, B, 3)))

            x2_v = x2scr[0:(GROUPS - 1) * GT * 128, :].rearrange("(g t p) e -> g p t e", t=GT, p=128)
            out_v = out[0:(GROUPS - 1) * GT * 128, :].rearrange("(g t p) e -> g p t e", t=GT, p=128)

            def group_of(v, whole, g):
                if isinstance(g, int) and g == GROUPS - 1:
                    return whole[g * GT * 128:TOK, :].rearrange("(t p) e -> p t e", p=128)
                return v[g]

            def load_group(g, p, k, part):
                if part != "norm":
                    return
                wait(sp, y_out[p], k * 16)
                sp.dma_start(xin[:, p, 0:tiles_of(g)], group_of(x2_v, x2scr, g)).then_inc(ln_in[p], 16)

            def store_group(g, p, k, nxt):
                nxt("norm")
                sp.wait_ge(y_ready, g + 1)
                sp.dma_start(group_of(out_v, out, g), y[:, p, 0:tiles_of(g)]).then_inc(y_out[p], 16)

            phase2(sp, load_group, store_group)
            for p in range(2):
                sp.wait_ge(y_out[p], 16 * len(range(p, GROUPS, 2)))

        @block.gpsimd
        def _(gp):
            nc.gpsimd.memset(ident[:], 0.0).then_inc(made, 1)
            nc.gpsimd.memset(lower[:], 1.0).then_inc(made, 1)
            gp.wait_ge(made, 2)
            nc.gpsimd.affine_select(out=ident[:], in_=ident[:], compare_op=ALU.not_equal, fill=1.0, base=0,
                                    pattern=[[-1, 128]], channel_multiplier=1).then_inc(made, 1)
            nc.gpsimd.affine_select(out=lower[:], in_=lower[:], compare_op=ALU.is_gt, fill=0.0, base=0,
                                    pattern=[[1, NE], [-1, NE]], channel_multiplier=0).then_inc(made, 1)

            def make_rstd(p, rows, n, inp, mid, outp, count):
                gp.wait_ge(inp, count)
                nc.gpsimd.tensor_tensor(vareps[0:rows, p, 0:n], meanvar[0:rows, p, 0:n, 1], eps_s[0:rows, 0:n], ALU.add).then_inc(mid, 1)
                gp.wait_ge(mid, count)
                nc.gpsimd.tensor_tensor(rstd[0:rows, p, 0:n], vareps[0:rows, p, 0:n], half_neg[0:rows, 0:n], ALU.pow).then_inc(outp, 1)

            def parts(full, rest, part, chain, done, n):
                nc.gpsimd.tensor_tensor(part[:, 0], full[:], zero[:, 0:1].unsqueeze(2).broadcast_to([128] + list(full.shape[1:])),
                                        ALU.add).then_inc(chain, 1)
                gp.wait_ge(chain, n * 2 + 1)
                nc.gpsimd.tensor_tensor(part[:, 1], full[:], part[:, 0], ALU.subtract)
                nc.gpsimd.tensor_tensor(rest[:], full[:], part[:, 0], ALU.subtract).then_inc(chain, 1)
                gp.wait_ge(chain, n * 2 + 2)
                nc.gpsimd.tensor_tensor(part[:, 2], rest[:], part[:, 1], ALU.subtract).then_inc(done, 1)

            gp.wait_ge(fills, 1)

            def group0(g, p, k):
                make_rstd(p, SQ, QG, meanvar_ready, vareps_ready, rstd_ready, g + 1)
                gp.wait_ge(qf_ready, 2 * g + 2)
                wait(gp, qscr_out[p], k * (QG * 16))
                wait(gp, qp_ready, g)
                parts(qf, qr, qp[:, p], q_chain, qp_ready, g)

            loop_groups0(gp, group0)
            gp.wait_ge(gbo_ready, 1)

            def step(bp, bm, be, bf):
                if be is not None:
                    gp.wait_ge(xr_in[be.buf], (be.round + 1) * 16)
                    wait(gp, x2_ready, be.n - 2)
                    nc.gpsimd.tensor_tensor(xb[:, be.buf], xr[:, be.buf], gbo[:], ALU.add).then_inc(xb_ready, 1)
                if bp is not None:
                    gp.wait_ge(k_ready, 2 * bp.n + 2)
                    wait(gp, kscr_out[bp.buf], bp.round * 16)
                    wait(gp, kp_ready, bp.n)
                    parts(kf, kr, kp[:, bp.buf], k_chain, kp_ready, bp.n)
                if be is not None:
                    gp.wait_ge(att0_ready, be.n + 1)
                    wait(gp, att_t_mm, be.n)
                    nc.gpsimd.tensor_tensor(att[:], att0[:], bv_s[:], ALU.add).then_inc(att_ready, 1)

            phase1(gp, step)

            def ln(g, p, k, part):
                if part == "norm":
                    make_rstd(p, 128, tiles_of(g), t_meanvar, t_vareps, t_rstd, g + 1)

            def ffn(g, p, k, nxt):
                n = tiles_of(g) * 128
                for j in range(NJ):
                    if j == 6:
                        nxt("norm")
                    if j < SHARED // HID:
                        gp.wait_ge(relu_ready, g * NJ + j + 1)
                        second = relu
                    else:
                        gp.wait_ge(gated_ready, g * NE + j - SHARED // HID + 1)
                        second = gated
                    wait(gp, down_mm, g * NJ + j - 1)
                    nc.gpsimd.tensor_tensor(sq[:, j % 2, 0:n], relu[:, j % 2, 0:n], second[:, j % 2, 0:n], ALU.mult).then_inc(sq_ready, 1)

            phase2(gp, ln, ffn)

        @block.scalar
        def _(act):
            act.wait_ge(consts, N_CONST)
            nc.scalar.activation(g_tanh[:], g_raw[:], ACT.Tanh).then_inc(gates_ready, 1)

            def group0(g, p, k):
                act.wait_ge(xnt_mm, g + 1)
                wait(act, q_mm, 2 * (g - 1))
                nc.scalar.activation(xnt[:, p, :, 0:QG * SQ], psum[:, 0:2, 0:QG * SQ], ACT.Copy).then_inc(xnt_ready, 1)
                for half in range(2):
                    act.wait_ge(q_mm, 2 * g + half + 1)
                    wait(act, qp_ready, g)
                    nc.scalar.activation(qf[:, half], psum[:, 2 + half, 0:QG * SQ], ACT.Identity,
                                         bias=bq_s[:, half:half + 1]).then_inc(qf_ready, 1)

            loop_groups0(act, group0)
            act.wait_ge(fills, 3)

            def step(bp, bm, be, bf):
                for i in range(UNITS):
                    if bp is not None and i in (1, 2):
                        half = i - 1
                        act.wait_ge(k_mm, 2 * bp.n + half + 1)
                        wait(act, kp_ready, bp.n)
                        nc.scalar.activation(kf[:, half], psum[:, (D0, D1)[half], 0:SK], ACT.Identity,
                                             bias=bk_s[:, half:half + 1]).then_inc(k_ready, 1)
                    if bf is not None and i == 5:
                        act.wait_ge(att_t_mm, bf.n + 1)
                        wait(act, o_mm, bf.n)
                        nc.scalar.activation(att_t[:], psum[:, D2, 0:CI * SQ].rearrange("p (c q) -> p c q", c=CI),
                                             ACT.Copy).then_inc(att_t_ready, 1)
                    if be is not None:
                        n = len(unit_pieces(i)) * SQ
                        act.wait_ge(score_mm, UNITS * be.n + i + 1)
                        wait(act, pv_mm, UNITS * (be.n - 1) + i + 1)
                        nc.scalar.activation(probs[0:KT, i, 0:n], psum[0:KT, SCORE_BANK[i % 2], 0:n], ACT.Exp,
                                             scale=SCALE).then_inc(exp_ready, 1)
                if bp is not None:
                    for t in range(NT):
                        act.wait_ge(v_mm, NT * bp.n + t + 1)
                        wait(act, pv_mm, UNITS * (bp.n - 2))
                        nc.scalar.activation(vs[0:KT, bp.buf, t, :, 0:D],
                                             psum[0:KT, (D2, D0, D1)[t], 0:E].rearrange("p (h d) -> p h d", h=H),
                                             ACT.Copy).then_inc(v_ready, 1)

            phase1(act, step)

            def ln(g, p, k, part):
                n = tiles_of(g)
                if part in range(n):
                    t = part
                    act.wait_ge(t_xnt_mm, g * GT + t + 1)
                    wait(act, up_mm, NJ * (g - 1))
                    nc.scalar.activation(xnt[:, p, :, t * 128:(t + 1) * 128],
                                         psum[:, LN_BANK, 0:CI * 128].rearrange("p (c q) -> p c q", c=CI),
                                         ACT.Copy).then_inc(t_xnt, 1)
                if part != "route":
                    return
                act.wait_ge(logit_mm, g + 1)
                wait(act, cw_ready, g)
                nc.scalar.activation(rt[:, 0, 0:n], psum[:, LOGIT_BANK, 0:n * NE].rearrange("p (t e) -> p t e", e=NE),
                                     ACT.Exp, scale=-1.0).then_inc(esig_ready, 1)

            def ffn(g, p, k, nxt):
                n = tiles_of(g) * 128
                for j in range(NJ):
                    act.wait_ge(up_mm, g * NJ + j + 1)
                    wait(act, sq_ready, g * NJ + j - 1)
                    nc.scalar.activation(relu[:, j % 2, 0:n], psum[:, UP_BANK[j % 2], 0:n], ACT.Relu).then_inc(relu_ready, 1)
                    if j >= 8:
                        nxt(j - 8)
                nxt("route")

            phase2(act, ln, ffn)

        @block.vector
        def _(dve):
            nc.vector.memset(half_neg[:], -0.5)
            nc.vector.memset(eps_s[:], EPS)
            nc.vector.memset(zero[:], 0.0).then_inc(fills, 1)
            nc.vector.memset(ks[ROWS:MROWS], 1.0).then_inc(fills, 1)
            nc.vector.memset(vs[:, :, :, :, D:DV], 1.0).then_inc(fills, 1)
            dve.wait_ge(consts, N_CONST)
            dve.wait_ge(gates_ready, 1)
            nc.vector.tensor_scalar(gbo[:], bo_s[:], g_tanh[0:SQ, 0:1], None, ALU.mult).then_inc(gbo_ready, 1)

            def normalise(p, rows, n, arrived, arrived_n, used, used_n, s_stats, s_mv, s_rstd, s_xn, g, width):
                dve.wait_ge(arrived, arrived_n)
                for i in range(n):
                    nc.vector.bn_stats(stats[0:rows, p, i], xin[0:rows, p, i]).then_inc(s_stats, 1)
                dve.wait_ge(s_stats, g * width + n)
                nc.vector.tensor_copy(carrier[0:rows], stats[0:rows, p, n - 1, 0:1])
                for i in range(n):
                    ins = nc.vector.bn_aggr(meanvar[0:rows, p, i], stats[0:rows, p, i])
                ins.then_inc(s_mv, 1)
                dve.wait_ge(s_rstd, g + 1)
                wait(dve, used, used_n)
                for i in range(n):
                    nc.vector.tensor_scalar(xn[0:rows, p, i], xin[0:rows, p, i], meanvar[0:rows, p, i, 0:1],
                                            rstd[0:rows, p, i:i + 1], ALU.subtract, ALU.mult).then_inc(s_xn, 1)

            def group0(g, p, k):
                normalise(p, SQ, QG, xin_in[p], k * 16 + 16, xnt_mm, g - 1,
                          stats_done, meanvar_ready, rstd_ready, xn_ready, g, QG)

            loop_groups0(dve, group0)

            def step(bp, bm, be, bf):
                for h in range(H):
                    if bm is not None:
                        dve.wait_ge(row_mm, H * bm.n + h + 1)
                        if h == 0:
                            wait(dve, mt_mm, bm.n)
                        nc.vector.tensor_reduce(negmax[:, h:h + 1], psum[0:SQ, ROW_BANK[h % 2], 0:SK],
                                                axis=AX_X, op=ALU.max, negate=True).then_inc(max_ready, 1)
                    if bf is not None and h == 8:
                        dve.wait_ge(o_mm, bf.n + 1)
                        dve.wait_ge(xb_ready, bf.n + 1)
                        wait(dve, x2_out[bf.buf], bf.round * 16)
                        nc.vector.scalar_tensor_tensor(out=x2[:, bf.buf], in0=psum[0:SQ, D1, 0:E], scalar=g_tanh[0:SQ, 0:1],
                                                       in1=xb[:, bf.buf], op0=ALU.mult, op1=ALU.add).then_inc(x2_ready, 1)
                if be is not None:
                    pv = psum[0:SQ, PV_BANK, 0:H * DV].rearrange("p (h d) -> p h d", d=DV)
                    dve.wait_ge(pv_mm, UNITS * (be.n + 1))
                    nc.vector.reciprocal(rden[:], pv[:, :, D]).then_inc(rden_ready, 1)
                    dve.wait_ge(rden_ready, be.n + 1)
                    wait(dve, att_ready, be.n)
                    nc.vector.tensor_tensor(att0[:].rearrange("p (h d) -> p h d", h=H), pv[:, :, 0:D],
                                            rden[:].unsqueeze(2).broadcast_to([SQ, H, D]), ALU.mult).then_inc(att0_ready, 1)
                if bm is not None:
                    dve.wait_ge(mt_mm, bm.n + 1)
                    if bm.c or not isinstance(bm.k, int) or bm.k:
                        prev = bm + -1
                        wait(dve, m_in[prev.buf], (prev.round + 1) * 32)
                    nc.vector.tensor_copy(mrow[:, 0], psum[0:H, D0, 0:SQ]).then_inc(mhi_ready, 1)
                    dve.wait_ge(mhi_ready, bm.n + 1)
                    nc.vector.tensor_tensor(mrow[:, 1], psum[0:H, D0, 0:SQ], mrow[:, 0], ALU.subtract).then_inc(mrow_ready, 1)

            phase1(dve, step)

            def route(g, p):
                n = tiles_of(g)
                done = [g * ROUTER_OPS]

                def link(ins):
                    done[0] = done[0] + 1
                    ins.then_inc(router, 1)
                    dve.wait_ge(router, done[0])

                esig, den, score, sfc = (rt[:, i, 0:n] for i in (0, 1, 2, 3))
                hi, lo, m1, m2 = (rt[:, i, 0:n, 0:4] for i in (4, 5, 6, 7))
                keep, masked, rank, w = (rt[:, i, 0:n] for i in (8, 9, 10, 11))
                halves = lambda v: v.rearrange("p t (g e) -> p t g e", g=2)
                dve.wait_ge(esig_ready, g + 1)
                link(nc.vector.tensor_scalar(den, esig, 1.0, None, ALU.add))
                link(nc.vector.reciprocal(score, den))
                link(nc.vector.tensor_tensor(sfc, score, gb_s[:].unsqueeze(1).broadcast_to([128, n, NE]), ALU.add))
                pair = sfc.rearrange("p t (q r) -> p t q r", r=2)
                link(nc.vector.tensor_tensor(hi, pair[:, :, :, 0], pair[:, :, :, 1], ALU.max))
                link(nc.vector.tensor_tensor(lo, pair[:, :, :, 0], pair[:, :, :, 1], ALU.min))
                two = lambda v: v.rearrange("p t (g r) -> p t g r", r=2)
                link(nc.vector.tensor_tensor(m1[:, :, 0:2], two(hi)[:, :, :, 0], two(hi)[:, :, :, 1], ALU.max))
                link(nc.vector.tensor_tensor(m1[:, :, 2:4], two(hi)[:, :, :, 0], two(hi)[:, :, :, 1], ALU.min))
                link(nc.vector.tensor_tensor(m2[:, :, 0:2], two(lo)[:, :, :, 0], two(lo)[:, :, :, 1], ALU.max))
                link(nc.vector.tensor_tensor(m2[:, :, 2:4], m1[:, :, 2:4], m2[:, :, 0:2], ALU.max))
                link(nc.vector.tensor_tensor(hi[:, :, 0:2], m1[:, :, 0:2], m2[:, :, 2:4], ALU.add))
                link(nc.vector.tensor_tensor(keep[:, :, 4:8], hi[:, :, 1:2].broadcast_to([128, n, 4]),
                                             hi[:, :, 0:1].broadcast_to([128, n, 4]), ALU.is_gt))
                link(nc.vector.tensor_scalar(keep[:, :, 0:4], keep[:, :, 4:8], -1.0, 1.0, ALU.mult, ALU.add))
                link(nc.vector.tensor_tensor(masked, sfc, keep, ALU.mult))
                mine = masked.unsqueeze(3).broadcast_to([128, n, NE, NE])
                other = masked.unsqueeze(2).broadcast_to([128, n, NE, NE])
                ge, gt = big[:, 0, 0:n], big[:, 1, 0:n]
                tie = lower[:].unsqueeze(1).broadcast_to([128, n, NE, NE])
                for t in range(n):
                    ins = nc.vector.tensor_tensor(ge[:, t], other[:, t], mine[:, t], ALU.is_equal)
                    ins2 = nc.vector.tensor_tensor(gt[:, t], other[:, t], mine[:, t], ALU.is_gt)
                link(ins2)
                link(nc.vector.tensor_tensor(ge, ge, tie, ALU.mult))
                link(nc.vector.tensor_tensor(gt, gt, ge, ALU.add))
                link(nc.vector.tensor_reduce(rank, gt, axis=AX_X, op=ALU.add))
                link(nc.vector.scalar_tensor_tensor(out=w, in0=rank, scalar=1.5, in1=score, op0=ALU.is_lt, op1=ALU.mult))
                link(nc.vector.tensor_reduce(den[:, :, 0:1], w, axis=AX_X, op=ALU.add))
                assert ROUTER_OPS == 19
                return w, den

            def ln(g, p, k, part):
                n = tiles_of(g)
                if part == "norm":
                    normalise(p, 128, n, ln_in[p], k * 16 + 16, t_xnt_mm, (g - 1) * GT,
                              t_stats, t_meanvar, t_rstd, t_xn, g, GT)
                if part != "route":
                    return
                w, den = route(g, p)
                nc.vector.tensor_scalar(rt[:, 4, 0:n, 0:1], den[:, :, 0:1], 1e-20, None, ALU.add).then_inc(norm_chain, 1)
                dve.wait_ge(norm_chain, 2 * g + 1)
                nc.vector.reciprocal(rt[:, 5, 0:n, 0:1], rt[:, 4, 0:n, 0:1]).then_inc(norm_chain, 1)
                dve.wait_ge(norm_chain, 2 * g + 2)
                wait(dve, cwb_mm, NE * (g - 1))
                nc.vector.scalar_tensor_tensor(out=cw[:, p, 0:n], in0=w, scalar=ROUTED_SCALE,
                                               in1=rt[:, 5, 0:n, 0:1].broadcast_to([128, n, NE]),
                                               op0=ALU.mult, op1=ALU.mult).then_inc(cw_ready, 1)

            def ffn(g, p, k, nxt):
                n = tiles_of(g)
                for j in range(NE):
                    dve.wait_ge(cwb_mm, g * NE + j + 1)
                    dve.wait_ge(relu_ready, g * NJ + SHARED // HID + j + 1)
                    wait(dve, sq_ready, g * NJ + SHARED // HID + j - 1)
                    nc.vector.tensor_tensor(gated[:, j % 2, 0:n * 128], relu[:, j % 2, 0:n * 128],
                                            psum[:, CWB_BANK[j % 2], 0:n * 128], ALU.mult).then_inc(gated_ready, 1)
                    if j == 1:
                        nxt("norm")
                dve.wait_ge(down_mm, (g + 1) * NJ)
                for t in range(0, n, 2):
                    m = min(2, n - t)
                    ins = nc.vector.scalar_tensor_tensor(
                        out=y[:, p, t:t + m].rearrange("p t e -> p (t e)"), in0=psum[:, DOWN_BANK + t // 2, 0:m * E],
                        scalar=g_tanh[:, 1:2], in1=xin[:, p, t:t + m].rearrange("p t e -> p (t e)"),
                        op0=ALU.mult, op1=ALU.add)
                ins.then_inc(y_ready, 1)
                nxt("route")

            phase2(dve, ln, ffn)

        @block.tensor
        def _(pe):
            mm = nc.tensor.matmul
            pe.wait_ge(consts, N_CONST)
            pe.wait_ge(made, 4)

            def group0(g, p, k):
                wait(pe, xnt_ready, g)
                for i in range(QG):
                    pe.wait_ge(xn_ready, g * QG + i + 1)
                    for c in range(CI):
                        ins = nc.tensor.transpose(psum[:, c, i * SQ:(i + 1) * SQ], xn[0:SQ, p, i, c * 128:(c + 1) * 128],
                                                  ident[0:SQ, 0:SQ])
                ins.then_inc(xnt_mm, 1)
                pe.wait_ge(xnt_ready, g + 1)
                wait(pe, qf_ready, 2 * g)
                for half in range(2):
                    for c in range(CI):
                        ins = mm(psum[:, 2 + half, 0:QG * SQ], wq_s[:, c, half * 128:(half + 1) * 128],
                                 xnt[:, p, c, 0:QG * SQ], start=(c == 0), stop=(c == CI - 1))
                    ins.then_inc(q_mm, 1)

            loop_groups0(pe, group0)
            pe.wait_ge(fills, 3)
            pe.wait_ge(xnt_ready, B // QG)
            pe.wait_ge(qf_ready, 2 * B // QG)

            def row_scores(b, h):
                wait(pe, max_ready, H * b.n + h - 1)
                if h == 0:
                    pe.wait_ge(qs_in[b.buf], (b.round + 1) * (6 * 16))
                    pe.wait_ge(ks_in[b.buf], (b.round + 1) * (3 * 16))
                mm(psum[0:SQ, ROW_BANK[h % 2], 0:SK], qs[0:ROWS, b.buf, h], ks[0:ROWS, b.buf, h],
                   start=True, stop=True).then_inc(row_mm, 1)

            def k_proj(b, half):
                if half == 0:
                    pe.wait_ge(ctx_in[b.buf], (b.round + 1) * 16)
                    wait(pe, mrow_ready, b.n - 1)
                    if isinstance(b.n, int) and b.n == 1:
                        pe.wait_ge(v_ready, 2)
                else:
                    wait(pe, v_ready, NT * b.n)
                for c in range(CI):
                    ins = mm(psum[:, (D0, D1)[half], 0:SK], wk_s[:, c, half * 128:(half + 1) * 128], ctxt[:, b.buf, c],
                             start=(c == 0), stop=(c == CI - 1))
                ins.then_inc(k_mm, 1)

            def v_proj(b, t):
                if t == 0:
                    wait(pe, att_t_ready, b.n - 2)
                    if isinstance(b.n, int) and 1 <= b.n <= 2:
                        pe.wait_ge(v_ready, NT * (b.n - 1) + 1)
                elif t == 1:
                    pe.wait_ge(k_ready, 2 * b.n + 1)
                else:
                    pe.wait_ge(k_ready, 2 * b.n + 2)
                    wait(pe, x2_ready, b.n - 2)
                for c in range(CI):
                    ins = mm(psum[0:KT, (D2, D0, D1)[t], 0:E], ctxt[:, b.buf, c, t * KSTEP:t * KSTEP + KT], wv_s[:, c],
                             start=(c == 0), stop=(c == CI - 1))
                ins.then_inc(v_mm, 1)

            def scores(b, u):
                wait(pe, exp_ready, UNITS * b.n + u - 1)
                if u == 0:
                    pe.wait_ge(m_in[b.buf], (b.round + 1) * 32)
                for h, t, col in unit_pieces(u):
                    ins = mm(psum[0:KT, SCORE_BANK[u % 2], col:col + SQ], ks[0:MROWS, b.buf, h, t * KSTEP:t * KSTEP + KT],
                             qs[0:MROWS, b.buf, h], start=True, stop=True)
                ins.then_inc(score_mm, 1)

            def times_v(b, u):
                pe.wait_ge(exp_ready, UNITS * b.n + u + 1)
                if u == 0:
                    pe.wait_ge(v_ready, NT * (b.n + 1))
                    wait(pe, att0_ready, b.n)
                for h, t, col in unit_pieces(u):
                    n = KT if t == NT - 1 else KSTEP
                    ins = mm(psum[0:SQ, PV_BANK, h * DV:(h + 1) * DV], probs[0:n, u, col:col + SQ],
                             vs[0:n, b.buf, t, h], start=(t == 0), stop=(t == NT - 1))
                ins.then_inc(pv_mm, 1)

            def att_transpose(b, v_count):
                pe.wait_ge(att_ready, b.n + 1)
                wait(pe, v_ready, v_count)
                for c in range(CI):
                    ins = nc.tensor.transpose(psum[:, D2, c * SQ:(c + 1) * SQ], att[:, c * 128:(c + 1) * 128], ident[0:SQ, 0:SQ])
                ins.then_inc(att_t_mm, 1)

            def out_proj(b, k_count):
                pe.wait_ge(att_t_ready, b.n + 1)
                wait(pe, k_ready, k_count)
                for c in range(CI):
                    ins = mm(psum[0:SQ, D1, 0:E], att_t[:, c], wo_s[:, c], start=(c == 0), stop=(c == CI - 1))
                ins.then_inc(o_mm, 1)

            def max_transpose(b, v_count):
                pe.wait_ge(max_ready, H * (b.n + 1))
                wait(pe, v_ready, v_count)
                nc.tensor.transpose(psum[0:H, D0, 0:SQ], negmax[:], ident[0:SQ, 0:SQ]).then_inc(mt_mm, 1)

            def step(bp, bm, be, bf):
                for i in range(H):
                    if bm is not None:
                        row_scores(bm, i)
                    if bp is not None and i < 2:
                        k_proj(bp, i)
                    if be is not None and i < UNITS:
                        scores(be, i)
                    if bf is not None and i == 4:
                        att_transpose(bf, NT * bp.n - 2 if bp is not None else NT * B)
                    if bf is not None and i == 7:
                        out_proj(bf, 2 * bp.n + 2 if bp is not None else 2 * B)
                    if be is not None and 0 <= i - 2 < UNITS:
                        times_v(be, i - 2)
                if bp is not None:
                    v_proj(bp, 0)
                    v_proj(bp, 1)
                if bm is not None:
                    max_transpose(bm, NT * bp.n + 2 if bp is not None else NT * B)
                if bp is not None:
                    v_proj(bp, 2)

            phase1(pe, step)
            pe.wait_ge(x2_ready, B)
            pe.wait_ge(att0_ready, B)

            def ln(g, p, k, part):
                n = tiles_of(g)
                if part in range(n):
                    t = part
                    pe.wait_ge(t_xn, g * GT + t + 1)
                    wait(pe, t_xnt, g * GT + t)
                    for c in range(CI):
                        ins = nc.tensor.transpose(psum[:, LN_BANK, c * 128:(c + 1) * 128],
                                                  xn[:, p, t, c * 128:(c + 1) * 128], ident[:])
                    ins.then_inc(t_xnt_mm, 1)
                if part != "route":
                    return
                pe.wait_ge(t_xnt, g * GT + n)
                wait(pe, esig_ready, g)
                for t in range(n):
                    for c in range(CI):
                        ins = mm(psum[:, LOGIT_BANK, t * NE:(t + 1) * NE], xnt[:, p, c, t * 128:(t + 1) * 128], gate_s[:, c],
                                 start=(c == 0), stop=(c == CI - 1))
                ins.then_inc(logit_mm, 1)

            def up(g, p, j):
                wait(pe, relu_ready, g * NJ + j - 1)
                n = tiles_of(g) * 128
                for c in range(CI):
                    ins = mm(psum[:, UP_BANK[j % 2], 0:n], up_s[:, c, j * HID:(j + 1) * HID], xnt[:, p, c, 0:n],
                             start=(c == 0), stop=(c == CI - 1))
                ins.then_inc(up_mm, 1)

            def spread_weights(g, p, j):
                if j == 0:
                    pe.wait_ge(cw_ready, g + 1)
                wait(pe, gated_ready, g * NE + j - 1)
                for t in range(tiles_of(g)):
                    ins = nc.tensor.transpose(psum[:, CWB_BANK[j % 2], t * 128:(t + 1) * 128],
                                              cw[:, p, t, j:j + 1].broadcast_to([128, 128]), ident[:])
                ins.then_inc(cwb_mm, 1)

            def down(g, p, j):
                pe.wait_ge(sq_ready, g * NJ + j + 1)
                if j == 0:
                    wait(pe, y_ready, g)
                for t in range(tiles_of(g)):
                    ins = mm(psum[:, DOWN_BANK + t // 2, (t % 2) * E:(t % 2 + 1) * E], sq[:, j % 2, t * 128:(t + 1) * 128],
                             down_s[:, j], start=(j == 0 and t % 2 == 0), stop=(j == NJ - 1), skip_group_check=True)
                ins.then_inc(down_mm, 1)

            def ffn(g, p, k, nxt):
                for j in range(NJ + 1):
                    if j < NJ:
                        up(g, p, j)
                        if j >= SHARED // HID:
                            spread_weights(g, p, j - SHARED // HID)
                    if j >= 1:
                        down(g, p, j - 1)
                    if j >= 8:
                        nxt(j - 8 if j < NJ else "route")

            phase2(pe, ln, ffn)


_ORDER = ("x", "ctx_t", "g_x", "g_f", "wq", "bq", "wk", "bk", "wv", "bv", "wo", "bo",
          "gate_t", "gate_b", "up_t", "down_t", "sup_t", "sdown_t")


def kernel(**inputs):
    import numpy as np
    import concourse.bacc as bacc
    from concourse.bass_utils import run_bass_kernel_spmd as run

    i = {k: np.asarray(v) for k, v in inputs.items()}

    def by_dim(w):
        return w.reshape(w.shape[:-1] + (H, D)).swapaxes(-1, -2).reshape(w.shape)

    laid = {
        "x": i["x"].reshape(TOK, E),
        "ctx_t": i["ctx_1024"].transpose(0, 2, 1),
        "g_x": i["g_xattn"], "g_f": i["g_ffn"],
        "wq": by_dim(i["L0_xattn_Wq"]), "bq": by_dim(i["L0_xattn_bq"]),
        "wk": by_dim(i["L0_xattn_Wk"]), "bk": by_dim(i["L0_xattn_bk"]),
        "wv": i["L0_xattn_Wv"], "bv": i["L0_xattn_bv"], "wo": i["L0_xattn_Wo"], "bo": i["L0_xattn_bo"],
        "gate_t": i["L0_ffn_gate_weight"].T, "gate_b": i["L0_ffn_gate_bias"],
        "up_t": i["L0_ffn_up_weights"].reshape(NE * HID, E).T,
        "down_t": i["L0_ffn_down_weights"].transpose(0, 2, 1).reshape(NE * HID, E),
        "sup_t": i["L0_ffn_shared_up_weight"].T, "sdown_t": i["L0_ffn_shared_down_weight"].T,
    }
    nc = bacc.Bacc("TRN2", target_bir_lowering=False, num_devices=1)
    arrays, args = {}, []
    for name in _ORDER:
        a = np.ascontiguousarray(laid[name])
        arrays[f"in_{name}"] = a
        args.append(nc.dram_tensor(f"in_{name}", a.shape, mybir.dt.from_np(a.dtype), kind="ExternalInput").ap())
    args.append(nc.dram_tensor("out_0", (TOK, E), F32, kind="ExternalOutput").ap())
    build(nc, *args)
    r = run(nc, [arrays], core_ids=[0])
    return r.results[0]["out_0"].reshape(B, SQ, E)
```

```python
from contextlib import ExitStack

import concourse.bass as bass
from concourse import mybir

F32 = mybir.dt.float32
BF16 = mybir.dt.bfloat16
ALU = mybir.AluOpType
ACT = mybir.ActivationFunctionType
AX_X = mybir.AxisListType.X

B, SQ, SK, E = 32, 100, 361, 256
H, D = 16, 16
CI = E // 128
TOK = B * SQ
NE, HID, SHARED = 8, 128, 512
NJ = NE + SHARED // HID
EPS = 1e-5
SCALE = float(D) ** -0.5
ROUTED_SCALE = 2.5
K_PARTS = (0, 1, 2, 0, 1, 0)
Q_PARTS = (0, 0, 0, 1, 1, 2)
ROWS = 6 * D
MROWS = ROWS + 2
KT = 121
KSTEP = 120
NT = 3
HPU = 4
UNITS = H // HPU * NT
DV = 2 * D
GT = 4
TILES = TOK // 128
GROUPS = -(-TILES // GT)
ROUTER_OPS = 19


def unit(u):
    return u // NT, u % NT


def upto(per, b, extra=0):
    n = per * b + extra
    return min(n, per * B) if isinstance(n, int) else n


def wait(eng, sem, value):
    if not (isinstance(value, int) and value <= 0):
        eng.wait_ge(sem, value)


class At:

    def __init__(self, k, c):
        self.k, self.c = k, c
        self.buf = c % 3
        self.round = k + c // 3
        self.n = k * 3 + c

    def __add__(self, d):
        return At(self.k, self.c + d)


def build(nc, x, ctx_t, g_x, g_f, wq, bq, wk, bk, wv, bv, wo, bo, gate_t, gate_b, up_t, down_t, sup_t, sdown_t, out):
    kscr = nc.dram_tensor("kscr", [B, 3, E, SK], BF16, kind="Internal").ap()
    qscr = nc.dram_tensor("qscr", [B, 3, E, SQ], BF16, kind="Internal").ap()
    x2scr = nc.dram_tensor("x2scr", [TOK, E], F32, kind="Internal").ap()

    with ExitStack() as ctx:
        def sb(name, shape, dt=F32):
            return ctx.enter_context(nc.sbuf_tensor(name, shape, dt))

        def sem(name):
            return ctx.enter_context(nc.semaphore(name))

        psum = ctx.enter_context(nc.psum_tensor("psum", [128, 8, 512], F32))

        ident = sb("ident", [128, 128])
        wq_s, wk_s, wv_s, wo_s = (sb(n, [128, CI, E]) for n in ("wq_s", "wk_s", "wv_s", "wo_s"))
        bq_s, bk_s = sb("bq_s", [128, 2]), sb("bk_s", [128, 2])
        bv_s, bo_s, gbo = sb("bv_s", [SQ, E]), sb("bo_s", [SQ, E]), sb("gbo", [SQ, E])
        up_s = sb("up_s", [128, CI, NJ * HID])
        down_s = sb("down_s", [128, NJ, E])
        gate_s = sb("gate_s", [128, CI, NE])
        gb_s = sb("gb_s", [128, NE])
        lower = sb("lower", [128, NE, NE])
        g_raw, g_tanh = sb("g_raw", [128, 2]), sb("g_tanh", [128, 2])
        half_neg = sb("half_neg", [128, GT])
        eps_s, zero = sb("eps_s", [128, GT]), sb("zero", [128, 1])

        xl = sb("xl", [SQ, 3, E])
        stats = sb("stats", [SQ, 3, 6])
        carrier = sb("carrier", [128, 1])
        meanvar = sb("meanvar", [SQ, 3, 2])
        vareps, rstd = sb("vareps", [SQ, 3]), sb("rstd", [SQ, 3])
        xn = sb("xn", [SQ, E])
        xnt = sb("xnt", [128, CI, SQ])
        qf, qr = sb("qf", [128, 2, SQ]), sb("qr", [128, 2, SQ])
        qp = sb("qp", [128, 3, 3, 2, SQ], BF16)
        ctxt = sb("ctxt", [128, 3, CI, SK])
        kf, kr = sb("kf", [128, 2, SK]), sb("kr", [128, 2, SK])
        kp = sb("kp", [128, 3, 3, 2, SK], BF16)
        ks = sb("ks", [128, 3, H, SK], BF16)
        qs = sb("qs", [128, 3, H, SQ], BF16)
        vs = sb("vs", [128, 3, NT, H, DV])
        negmax = sb("negmax", [SQ, H])
        mrow = sb("mrow", [H, 2, SQ], BF16)
        probs = sb("probs", [128, UNITS, HPU * SQ])
        pvt = sb("pvt", [128, HPU * SQ])
        rden = sb("rden", [SQ, H])
        att0, att = sb("att0", [SQ, E]), sb("att", [SQ, E])
        att_t = sb("att_t", [128, CI, SQ])
        xr = sb("xr", [SQ, 3, E])
        xb = sb("xb", [SQ, 3, E])
        x2 = sb("x2", [SQ, 3, E])

        xin2 = sb("xin2", [128, 2, GT, E])
        xn2 = sb("xn2", [128, 2, GT, E])
        xnt2 = sb("xnt2", [128, 2, CI, GT * 128])
        stats2 = sb("stats2", [128, 2, GT, 6])
        meanvar2 = sb("meanvar2", [128, 2, GT, 2])
        vareps2, rstd2 = sb("vareps2", [128, 2, GT]), sb("rstd2", [128, 2, GT])
        spare = probs[:].rearrange("p u n -> p (u n)")
        relu, gated = (spare[:, i * GT * E:(i + 1) * GT * E].rearrange("p (a n) -> p a n", a=2) for i in (2, 3))
        sq = sb("sq", [128, 2, GT * 128])
        cw = sb("cw", [128, 2, GT, NE])
        rt = sb("rt", [128, 12, GT, NE])
        big = sb("big", [128, 2, GT, NE, NE])
        y = probs[:].rearrange("p u n -> p (u n)")[:, 0:2 * GT * E].rearrange("p (a t e) -> p a t e", a=2, t=GT)

        consts = sem("consts")
        made = sem("made")
        fills = sem("fills")
        gates_ready = sem("gates_ready")
        gbo_ready = sem("gbo_ready")
        xl_in = [sem(f"xl_in{i}") for i in range(3)]
        stats_done, meanvar_ready, vareps_ready = sem("stats_done"), sem("meanvar_ready"), sem("vareps_ready")
        rstd_ready, xn_ready = sem("rstd_ready"), sem("xn_ready")
        xnt_mm, xnt_ready = sem("xnt_mm"), sem("xnt_ready")
        q_mm, q_ready, q_chain, qp_ready = sem("q_mm"), sem("q_ready"), sem("q_chain"), sem("qp_ready")
        qscr_out = [sem(f"qscr_out{i}") for i in range(3)]

        ctx_in = [sem(f"ctx_in{i}") for i in range(3)]
        xr_in = [sem(f"xr_in{i}") for i in range(3)]
        qs_in = [sem(f"qs_in{i}") for i in range(3)]
        ks_in = [sem(f"ks_in{i}") for i in range(3)]
        m_in = [sem(f"m_in{i}") for i in range(3)]
        kscr_out = [sem(f"kscr_out{i}") for i in range(3)]
        x2_out = [sem(f"x2_out{i}") for i in range(3)]
        k_mm, k_ready, kr_ready, k_chain, kp_ready = (
            sem("k_mm"), sem("k_ready"), sem("kr_ready"), sem("k_chain"), sem("kp_ready"))
        v_mm, v_ready = sem("v_mm"), sem("v_ready")
        row_mm, max_ready, mt_mm, mhi_ready, mrow_ready = (
            sem("row_mm"), sem("max_ready"), sem("mt_mm"), sem("mhi_ready"), sem("mrow_ready"))
        score_mm, exp_ready, pv_mm = sem("score_mm"), sem("exp_ready"), sem("pv_mm")
        pvt_ready, pvt_mm = sem("pvt_ready"), sem("pvt_mm")
        rden_ready, att0_ready, att_ready = sem("rden_ready"), sem("att0_ready"), sem("att_ready")
        att_t_mm, att_t_ready, o_mm, xb_ready, x2_ready = (
            sem("att_t_mm"), sem("att_t_ready"), sem("o_mm"), sem("xb_ready"), sem("x2_ready"))

        ln_in = [sem(f"ln_in{i}") for i in range(2)]
        t_stats, t_meanvar, t_vareps, t_rstd, t_xn = (
            sem("t_stats"), sem("t_meanvar"), sem("t_vareps"), sem("t_rstd"), sem("t_xn"))
        t_xnt_mm, t_xnt = sem("t_xnt_mm"), sem("t_xnt")
        logit_mm, esig_ready, router, cw_ready = sem("logit_mm"), sem("esig_ready"), sem("router"), sem("cw_ready")
        up_mm, relu_ready, cwb_mm, gated_ready, sq_ready, down_mm = (
            sem("up_mm"), sem("relu_ready"), sem("cwb_mm"), sem("gated_ready"), sem("sq_ready"), sem("down_mm"))
        norm_chain = sem("norm_chain")
        y_ready = sem("y_ready")
        y_out = [sem(f"y_out{i}") for i in range(2)]

        N_CONST = 18 * 16

        ROW_BANK, SCORE_BANK, PV_BANK, D0, D1, D2 = (0, 1), (2, 3), 4, 5, 6, 7
        UP_BANK, CWB_BANK, DOWN_BANK, LN_BANK, LOGIT_BANK = (0, 1), (2, 3), 4, 6, 7

        def phase1(eng, do):
            def edge(s):
                do(*(At((s + d) // 3, (s + d) % 3) if 0 <= s + d < B else None for d in (3, 2, 1, 0, -1)))

            loops = (B - 4) // 3 + 1
            for s in range(-3, 3):
                edge(s)
            with eng.Fori(1, loops - 1) as k:
                for c in range(3):
                    do(*(At(k, c + d) for d in (3, 2, 1, 0, -1)))
            for s in range(3 * (loops - 1), B + 1):
                edge(s)

        def tiles_of(g):
            return min(GT, TILES - g * GT) if isinstance(g, int) else GT

        def phase2(eng, ln, ffn):
            def whole(g, p, k):
                for part in ("norm", 0, 1, 2, 3, "route"):
                    ln(g, p, k, part)

            def ahead(g, p, k):
                return lambda part: ln(g, p, k, part)

            whole(0, 0, 0)
            ffn(0, 0, 0, ahead(1, 1, 0))
            with eng.Fori(0, 2) as k:
                ffn(k * 2 + 1, 1, k, ahead(k * 2 + 2, 0, k + 1))
                ffn(k * 2 + 2, 0, k + 1, ahead(k * 2 + 3, 1, k + 1))
            ffn(5, 1, 2, ahead(6, 0, 3))
            ffn(6, 0, 3, lambda part: None)

        block = ctx.enter_context(nc.Block())

        @block.sync
        def _(sp):
            for dst, src in (
                (wq_s, wq.rearrange("(c p) n -> p c n", p=128)), (wk_s, wk.rearrange("(c p) n -> p c n", p=128)),
                (wv_s, wv.rearrange("(c p) n -> p c n", p=128)), (wo_s, wo.rearrange("(c p) n -> p c n", p=128)),
                (bv_s, bv.partition_broadcast(SQ)), (bo_s, bo.partition_broadcast(SQ)),
                (gb_s, gate_b.partition_broadcast(128)),
                (gate_s, gate_t.rearrange("(c p) n -> p c n", p=128)),
            ):
                sp.dma_start(dst[:], src).then_inc(consts, 16)
            for half in range(2):
                sp.dma_start(bq_s[:, half:half + 1], bq.rearrange("(a p o) -> a p o", p=128, o=1)[half]).then_inc(consts, 16)
                sp.dma_start(bk_s[:, half:half + 1], bk.rearrange("(a p o) -> a p o", p=128, o=1)[half]).then_inc(consts, 16)
            for n, g in enumerate((g_x, g_f)):
                sp.dma_start(g_raw[:, n:n + 1], g.partition_broadcast(128)).then_inc(consts, 16)
            sp.dma_start(up_s[:, :, 0:SHARED], sup_t.rearrange("(c p) n -> p c n", p=128)).then_inc(consts, 16)
            sp.dma_start(up_s[:, :, SHARED:], up_t.rearrange("(c p) n -> p c n", p=128)).then_inc(consts, 16)
            sp.dma_start(down_s[:, 0:SHARED // HID, :], sdown_t.rearrange("(j p) n -> p j n", p=HID)).then_inc(consts, 16)
            sp.dma_start(down_s[:, SHARED // HID:, :], down_t.rearrange("(j p) n -> p j n", p=HID)).then_inc(consts, 16)

            def load_ahead(b):
                wait(sp, v_mm, NT * (b.n - 2))
                sp.dma_start(ctxt[:, b.buf], ctx_t[b.n].rearrange("(c p) n -> p c n", p=128)).then_inc(ctx_in[b.buf], 16)
                wait(sp, xn_ready, b.n - 2)
                sp.dma_start(xl[:, b.buf], x[bass.ds(b.n * SQ, SQ), :]).then_inc(xl_in[b.buf], 16)

            def step(bl, bv, bm, be, bf):
                if bl is not None and not (isinstance(bl.n, int) and bl.n + 1 >= B):
                    load_ahead(bl + 1)
                if bv is not None:
                    wait(sp, score_mm, UNITS * (bv.n - 2))
                    sp.wait_ge(kscr_out[bv.buf], (bv.round + 1) * 16)
                    kv = kscr[bv.n].rearrange("r (d h) k -> (r d) (h k)", h=H)
                    for lo, n in ((0, 3), (3, 2), (5, 1)):
                        sp.dma_start(ks[lo * D:(lo + n) * D, bv.buf], kv[0:n * D].rearrange("p (h k) -> p h k", h=H)).then_inc(ks_in[bv.buf], 16)
                    sp.wait_ge(qscr_out[bv.buf], (bv.round + 1) * 16)
                    for r in range(6):
                        sp.dma_start(qs[r * D:(r + 1) * D, bv.buf],
                                     qscr[bv.n, Q_PARTS[r]].rearrange("(d h) q -> d h q", h=H)).then_inc(qs_in[bv.buf], 16)
                if bm is not None:
                    wait(sp, xb_ready, bm.n - 2)
                    sp.dma_start(xr[:, bm.buf], x[bass.ds(bm.n * SQ, SQ), :]).then_inc(xr_in[bm.buf], 16)
                if bl is not None:
                    sp.wait_ge(kp_ready, bl.n + 1)
                    sp.dma_start(kscr[bl.n].rearrange("r (a p) k -> p r a k", p=128), kp[:, bl.buf]).then_inc(kscr_out[bl.buf], 16)
                    sp.wait_ge(qp_ready, bl.n + 1)
                    sp.dma_start(qscr[bl.n].rearrange("r (a p) q -> p r a q", p=128), qp[:, bl.buf]).then_inc(qscr_out[bl.buf], 16)
                if bf is not None:
                    sp.wait_ge(x2_ready, bf.n + 1)
                    sp.dma_start(x2scr[bass.ds(bf.n * SQ, SQ), :], x2[:, bf.buf]).then_inc(x2_out[bf.buf], 16)
                if bm is not None:
                    sp.wait_ge(mrow_ready, bm.n + 1)
                    for r in range(2):
                        sp.dma_start(qs[ROWS + r:ROWS + r + 1, bm.buf], mrow[:, r, :]).then_inc(m_in[bm.buf], 16)

            load_ahead(At(0, 0))
            phase1(sp, step)
            for i in range(3):
                sp.wait_ge(x2_out[i], 16 * len(range(i, B, 3)))

            x2_v = x2scr[0:(GROUPS - 1) * GT * 128, :].rearrange("(g t p) e -> g p t e", t=GT, p=128)
            out_v = out[0:(GROUPS - 1) * GT * 128, :].rearrange("(g t p) e -> g p t e", t=GT, p=128)

            def group_of(v, whole, g):
                if isinstance(g, int) and g == GROUPS - 1:
                    return whole[g * GT * 128:TOK, :].rearrange("(t p) e -> p t e", p=128)
                return v[g]

            def load_group(g, p, k, part):
                if part != "norm":
                    return
                wait(sp, y_out[p], k * 16)
                sp.dma_start(xin2[:, p, 0:tiles_of(g)], group_of(x2_v, x2scr, g)).then_inc(ln_in[p], 16)

            def store_group(g, p, k, nxt):
                nxt("norm")
                sp.wait_ge(y_ready, g + 1)
                sp.dma_start(group_of(out_v, out, g), y[:, p, 0:tiles_of(g)]).then_inc(y_out[p], 16)

            phase2(sp, load_group, store_group)
            for p in range(2):
                sp.wait_ge(y_out[p], 16 * len(range(p, GROUPS, 2)))

        @block.gpsimd
        def _(gp):
            nc.gpsimd.memset(ident[:], 0.0).then_inc(made, 1)
            nc.gpsimd.memset(lower[:], 1.0).then_inc(made, 1)
            gp.wait_ge(made, 2)
            nc.gpsimd.affine_select(out=ident[:], in_=ident[:], compare_op=ALU.not_equal, fill=1.0, base=0,
                                    pattern=[[-1, 128]], channel_multiplier=1).then_inc(made, 1)
            nc.gpsimd.affine_select(out=lower[:], in_=lower[:], compare_op=ALU.is_gt, fill=0.0, base=0,
                                    pattern=[[1, NE], [-1, NE]], channel_multiplier=0).then_inc(made, 1)

            def make_rstd(mv, ve, rs, rows, n, inp, mid, outp, count):
                gp.wait_ge(inp, count)
                nc.gpsimd.tensor_tensor(ve, mv, eps_s[0:rows, 0:n], ALU.add).then_inc(mid, 1)
                gp.wait_ge(mid, count)
                nc.gpsimd.tensor_tensor(rs, ve, half_neg[0:rows, 0:n], ALU.pow).then_inc(outp, 1)

            gp.wait_ge(fills, 1)
            gp.wait_ge(gbo_ready, 1)

            def step(bl, bv, bm, be, bf):
                if bl is not None:
                    b = bl.buf
                    make_rstd(meanvar[:, b, 1:2], vareps[:, b:b + 1], rstd[:, b:b + 1], SQ, 1,
                              meanvar_ready, vareps_ready, rstd_ready, bl.n + 1)
                if bf is not None:
                    gp.wait_ge(att0_ready, bf.n + 1)
                    wait(gp, att_t_mm, bf.n)
                    nc.gpsimd.tensor_tensor(att[:], att0[:], bv_s[:], ALU.add).then_inc(att_ready, 1)
                if bl is not None:
                    gp.wait_ge(k_ready, 2 * bl.n + 2)
                    nc.gpsimd.tensor_tensor(kp[:, b, 1], kf[:], kp[:, b, 0], ALU.subtract).then_inc(k_chain, 1)
                    gp.wait_ge(kr_ready, bl.n + 1)
                    gp.wait_ge(k_chain, bl.n + 1)
                    nc.gpsimd.tensor_tensor(kp[:, b, 2], kr[:], kp[:, b, 1], ALU.subtract).then_inc(kp_ready, 1)
                    gp.wait_ge(q_ready, bl.n + 1)
                    nc.gpsimd.tensor_tensor(qp[:, b, 1], qf[:], qp[:, b, 0], ALU.subtract)
                    nc.gpsimd.tensor_tensor(qr[:], qf[:], qp[:, b, 0], ALU.subtract).then_inc(q_chain, 1)
                    gp.wait_ge(q_chain, bl.n + 1)
                    nc.gpsimd.tensor_tensor(qp[:, b, 2], qr[:], qp[:, b, 1], ALU.subtract).then_inc(qp_ready, 1)
                if be is not None:
                    gp.wait_ge(xr_in[be.buf], (be.round + 1) * 16)
                    wait(gp, x2_ready, be.n - 2)
                    wait(gp, x2_out[be.buf], be.round * 16)
                    nc.gpsimd.tensor_tensor(xb[:, be.buf], xr[:, be.buf], gbo[:], ALU.add).then_inc(xb_ready, 1)

            phase1(gp, step)

            def ln(g, p, k, part):
                if part == "norm":
                    n = tiles_of(g)
                    make_rstd(meanvar2[:, p, 0:n, 1], vareps2[:, p, 0:n], rstd2[:, p, 0:n], 128, n,
                              t_meanvar, t_vareps, t_rstd, g + 1)

            def ffn(g, p, k, nxt):
                n = tiles_of(g) * 128
                for j in range(NJ):
                    if j == 6:
                        nxt("norm")
                    if j < SHARED // HID:
                        gp.wait_ge(relu_ready, g * NJ + j + 1)
                        second = relu
                    else:
                        gp.wait_ge(gated_ready, g * NE + j - SHARED // HID + 1)
                        second = gated
                    wait(gp, down_mm, g * NJ + j - 1)
                    nc.gpsimd.tensor_tensor(sq[:, j % 2, 0:n], relu[:, j % 2, 0:n], second[:, j % 2, 0:n], ALU.mult).then_inc(sq_ready, 1)

            phase2(gp, ln, ffn)

        @block.scalar
        def _(act):
            act.wait_ge(consts, N_CONST)
            nc.scalar.activation(g_tanh[:], g_raw[:], ACT.Tanh).then_inc(gates_ready, 1)

            act.wait_ge(fills, 3)

            def exp_unit(be, i):
                act.wait_ge(score_mm, UNITS * be.n + i + 1)
                wait(act, pv_mm, UNITS * (be.n - 1) + i + 1)
                nc.scalar.activation(probs[0:KT, i], psum[0:KT, SCORE_BANK[i % 2], 0:HPU * SQ], ACT.Exp,
                                     scale=SCALE).then_inc(exp_ready, 1)

            def split_first(full, part, bank, bias, done):
                nc.scalar.activation(full, bank, ACT.Identity, bias=bias)
                ins = nc.scalar.activation(part, bank, ACT.Identity, bias=bias)
                if done is not None:
                    ins.then_inc(done, 1)

            def step(bl, bv, bm, be, bf):
                for i in range(H):
                    if bl is not None and i < 2:
                        act.wait_ge(k_mm, 2 * bl.n + i + 1)
                        wait(act, kp_ready, bl.n)
                        wait(act, kscr_out[bl.buf], bl.round * 16)
                        split_first(kf[:, i], kp[:, bl.buf, 0, i], psum[:, (D0, D1)[i], 0:SK], bk_s[:, i:i + 1], k_ready)
                    if be is not None and 2 <= i < 2 + UNITS:
                        exp_unit(be, i - 2)
                    if bl is not None and i == 4:
                        act.wait_ge(xnt_mm, bl.n + 1)
                        wait(act, q_mm, bl.n)
                        nc.scalar.activation(xnt[:], psum[:, D2, 0:CI * SQ].rearrange("p (c q) -> p c q", c=CI),
                                             ACT.Copy).then_inc(xnt_ready, 1)
                    if bf is not None and i == 6:
                        act.wait_ge(att_t_mm, bf.n + 1)
                        wait(act, o_mm, bf.n)
                        nc.scalar.activation(att_t[:], psum[:, D0, 0:CI * SQ].rearrange("p (c q) -> p c q", c=CI),
                                             ACT.Copy).then_inc(att_t_ready, 1)
                    if bl is not None and i == 7:
                        act.wait_ge(q_mm, bl.n + 1)
                        wait(act, qp_ready, bl.n)
                        wait(act, qscr_out[bl.buf], bl.round * 16)
                        for half in range(2):
                            split_first(qf[:, half], qp[:, bl.buf, 0, half], psum[:, D2, half * SQ:(half + 1) * SQ],
                                        bq_s[:, half:half + 1], q_ready if half else None)
                if be is not None:
                    act.wait_ge(pv_mm, UNITS * (be.n + 1))
                    wait(act, pvt_mm, be.n)
                    nc.scalar.activation(pvt[:], psum[:, PV_BANK, 0:HPU * SQ], ACT.Copy).then_inc(pvt_ready, 1)
                if bv is not None:
                    for t in range(NT):
                        act.wait_ge(v_mm, NT * bv.n + t + 1)
                        wait(act, pv_mm, UNITS * (bv.n - 2))
                        nc.scalar.activation(vs[0:KT, bv.buf, t, :, 0:D],
                                             psum[0:KT, (D2, D1, D2)[t], 0:E].rearrange("p (h d) -> p h d", h=H),
                                             ACT.Copy).then_inc(v_ready, 1)

            phase1(act, step)

            def ln(g, p, k, part):
                n = tiles_of(g)
                if part in range(n):
                    t = part
                    act.wait_ge(t_xnt_mm, g * GT + t + 1)
                    wait(act, up_mm, NJ * (g - 1))
                    nc.scalar.activation(xnt2[:, p, :, t * 128:(t + 1) * 128],
                                         psum[:, LN_BANK, 0:CI * 128].rearrange("p (c q) -> p c q", c=CI),
                                         ACT.Copy).then_inc(t_xnt, 1)
                if part != "route":
                    return
                act.wait_ge(logit_mm, g + 1)
                wait(act, cw_ready, g)
                nc.scalar.activation(rt[:, 0, 0:n], psum[:, LOGIT_BANK, 0:n * NE].rearrange("p (t e) -> p t e", e=NE),
                                     ACT.Exp, scale=-1.0).then_inc(esig_ready, 1)

            def ffn(g, p, k, nxt):
                n = tiles_of(g) * 128
                for j in range(NJ):
                    act.wait_ge(up_mm, g * NJ + j + 1)
                    wait(act, sq_ready, g * NJ + j - 1)
                    nc.scalar.activation(relu[:, j % 2, 0:n], psum[:, UP_BANK[j % 2], 0:n], ACT.Relu).then_inc(relu_ready, 1)
                    if j >= 8:
                        nxt(j - 8)
                nxt("route")

            phase2(act, ln, ffn)

        @block.vector
        def _(dve):
            nc.vector.memset(half_neg[:], -0.5)
            nc.vector.memset(eps_s[:], EPS)
            nc.vector.memset(zero[:], 0.0).then_inc(fills, 1)
            nc.vector.memset(ks[ROWS:MROWS], 1.0).then_inc(fills, 1)
            nc.vector.memset(vs[:, :, :, :, D:DV], 1.0).then_inc(fills, 1)
            dve.wait_ge(consts, N_CONST)
            dve.wait_ge(gates_ready, 1)
            nc.vector.tensor_scalar(gbo[:], bo_s[:], g_tanh[0:SQ, 0:1], None, ALU.mult).then_inc(gbo_ready, 1)

            def aggregate(last, source, rows, seen, count):
                dve.wait_ge(seen, count)
                nc.vector.tensor_copy(carrier[0:rows], last)
                for out_ap, in_ap in source:
                    ins = nc.vector.bn_aggr(out_ap, in_ap)
                return ins

            def step(bl, bv, bm, be, bf):
                for h in range(H):
                    if bm is not None:
                        dve.wait_ge(row_mm, H * bm.n + h + 1)
                        if h == 0:
                            wait(dve, mt_mm, bm.n)
                        nc.vector.tensor_reduce(negmax[:, h:h + 1], psum[0:SQ, ROW_BANK[h % 2], 0:SK],
                                                axis=AX_X, op=ALU.max, negate=True).then_inc(max_ready, 1)
                    if bl is not None and h == 0:
                        b = bl.buf
                        dve.wait_ge(xl_in[b], (bl.round + 1) * 16)
                        nc.vector.bn_stats(stats[:, b], xl[:, b]).then_inc(stats_done, 1)
                        aggregate(stats[:, b, 0:1], [(meanvar[:, b], stats[:, b])], SQ, stats_done,
                                  bl.n + 1).then_inc(meanvar_ready, 1)
                    if bl is not None and h == 2:
                        dve.wait_ge(rstd_ready, bl.n + 1)
                        wait(dve, xnt_mm, bl.n)
                        nc.vector.tensor_scalar(xn[:], xl[:, b], meanvar[:, b, 0:1], rstd[:, b:b + 1],
                                                ALU.subtract, ALU.mult).then_inc(xn_ready, 1)
                    if bf is not None and h == 3:
                        pv = psum[0:SQ, D2, :].rearrange("p (h r) -> p h r", r=DV)
                        dve.wait_ge(pvt_mm, bf.n + 1)
                        nc.vector.reciprocal(rden[:], pv[:, :, D]).then_inc(rden_ready, 1)
                        dve.wait_ge(rden_ready, bf.n + 1)
                        wait(dve, att_ready, bf.n)
                        nc.vector.tensor_tensor(att0[:].rearrange("p (h d) -> p h d", h=H), pv[:, :, 0:D],
                                                rden[:].unsqueeze(2).broadcast_to([SQ, H, D]), ALU.mult).then_inc(att0_ready, 1)
                    if bl is not None and h == 4:
                        dve.wait_ge(k_ready, 2 * bl.n + 2)
                        wait(dve, kp_ready, bl.n)
                        nc.vector.tensor_tensor(kr[:], kf[:], kp[:, b, 0], ALU.subtract).then_inc(kr_ready, 1)
                    if bf is not None and h == 10:
                        dve.wait_ge(o_mm, bf.n + 1)
                        dve.wait_ge(xb_ready, bf.n + 1)
                        nc.vector.scalar_tensor_tensor(out=x2[:, bf.buf], in0=psum[0:SQ, D1, 0:E], scalar=g_tanh[0:SQ, 0:1],
                                                       in1=xb[:, bf.buf], op0=ALU.mult, op1=ALU.add).then_inc(x2_ready, 1)
                if bm is not None:
                    dve.wait_ge(mt_mm, bm.n + 1)
                    prev = bm + -1
                    wait(dve, m_in[prev.buf], (prev.round + 1) * 32)
                    nc.vector.tensor_copy(mrow[:, 0], psum[0:H, D0, 0:SQ]).then_inc(mhi_ready, 1)
                    dve.wait_ge(mhi_ready, bm.n + 1)
                    nc.vector.tensor_tensor(mrow[:, 1], psum[0:H, D0, 0:SQ], mrow[:, 0], ALU.subtract).then_inc(mrow_ready, 1)

            phase1(dve, step)

            def route(g, p):
                n = tiles_of(g)
                done = [g * ROUTER_OPS]

                def link(ins):
                    done[0] = done[0] + 1
                    ins.then_inc(router, 1)
                    dve.wait_ge(router, done[0])

                esig, den, score, sfc = (rt[:, i, 0:n] for i in (0, 1, 2, 3))
                hi, lo, m1, m2 = (rt[:, i, 0:n, 0:4] for i in (4, 5, 6, 7))
                keep, masked, rank, w = (rt[:, i, 0:n] for i in (8, 9, 10, 11))
                halves = lambda v: v.rearrange("p t (g e) -> p t g e", g=2)
                dve.wait_ge(esig_ready, g + 1)
                link(nc.vector.tensor_scalar(den, esig, 1.0, None, ALU.add))
                link(nc.vector.reciprocal(score, den))
                link(nc.vector.tensor_tensor(sfc, score, gb_s[:].unsqueeze(1).broadcast_to([128, n, NE]), ALU.add))
                pair = sfc.rearrange("p t (q r) -> p t q r", r=2)
                link(nc.vector.tensor_tensor(hi, pair[:, :, :, 0], pair[:, :, :, 1], ALU.max))
                link(nc.vector.tensor_tensor(lo, pair[:, :, :, 0], pair[:, :, :, 1], ALU.min))
                two = lambda v: v.rearrange("p t (g r) -> p t g r", r=2)
                link(nc.vector.tensor_tensor(m1[:, :, 0:2], two(hi)[:, :, :, 0], two(hi)[:, :, :, 1], ALU.max))
                link(nc.vector.tensor_tensor(m1[:, :, 2:4], two(hi)[:, :, :, 0], two(hi)[:, :, :, 1], ALU.min))
                link(nc.vector.tensor_tensor(m2[:, :, 0:2], two(lo)[:, :, :, 0], two(lo)[:, :, :, 1], ALU.max))
                link(nc.vector.tensor_tensor(m2[:, :, 2:4], m1[:, :, 2:4], m2[:, :, 0:2], ALU.max))
                link(nc.vector.tensor_tensor(hi[:, :, 0:2], m1[:, :, 0:2], m2[:, :, 2:4], ALU.add))
                link(nc.vector.tensor_tensor(keep[:, :, 4:8], hi[:, :, 1:2].broadcast_to([128, n, 4]),
                                             hi[:, :, 0:1].broadcast_to([128, n, 4]), ALU.is_gt))
                link(nc.vector.tensor_scalar(keep[:, :, 0:4], keep[:, :, 4:8], -1.0, 1.0, ALU.mult, ALU.add))
                link(nc.vector.tensor_tensor(masked, sfc, keep, ALU.mult))
                mine = masked.unsqueeze(3).broadcast_to([128, n, NE, NE])
                other = masked.unsqueeze(2).broadcast_to([128, n, NE, NE])
                ge, gt = big[:, 0, 0:n], big[:, 1, 0:n]
                tie = lower[:].unsqueeze(1).broadcast_to([128, n, NE, NE])
                for t in range(n):
                    ins = nc.vector.tensor_tensor(ge[:, t], other[:, t], mine[:, t], ALU.is_equal)
                    ins2 = nc.vector.tensor_tensor(gt[:, t], other[:, t], mine[:, t], ALU.is_gt)
                link(ins2)
                link(nc.vector.tensor_tensor(ge, ge, tie, ALU.mult))
                link(nc.vector.tensor_tensor(gt, gt, ge, ALU.add))
                link(nc.vector.tensor_reduce(rank, gt, axis=AX_X, op=ALU.add))
                link(nc.vector.scalar_tensor_tensor(out=w, in0=rank, scalar=1.5, in1=score, op0=ALU.is_lt, op1=ALU.mult))
                link(nc.vector.tensor_reduce(den[:, :, 0:1], w, axis=AX_X, op=ALU.add))
                assert ROUTER_OPS == 19
                return w, den

            def ln(g, p, k, part):
                n = tiles_of(g)
                if part == "norm":
                    dve.wait_ge(ln_in[p], k * 16 + 16)
                    for t in range(n):
                        nc.vector.bn_stats(stats2[:, p, t], xin2[:, p, t]).then_inc(t_stats, 1)
                    aggregate(stats2[:, p, n - 1, 0:1], [(meanvar2[:, p, t], stats2[:, p, t]) for t in range(n)], 128,
                              t_stats, g * GT + n).then_inc(t_meanvar, 1)
                    dve.wait_ge(t_rstd, g + 1)
                    wait(dve, t_xnt_mm, (g - 1) * GT)
                    for t in range(n):
                        nc.vector.tensor_scalar(xn2[:, p, t], xin2[:, p, t], meanvar2[:, p, t, 0:1], rstd2[:, p, t:t + 1],
                                                ALU.subtract, ALU.mult).then_inc(t_xn, 1)
                if part != "route":
                    return
                w, den = route(g, p)
                nc.vector.tensor_scalar(rt[:, 4, 0:n, 0:1], den[:, :, 0:1], 1e-20, None, ALU.add).then_inc(norm_chain, 1)
                dve.wait_ge(norm_chain, 2 * g + 1)
                nc.vector.reciprocal(rt[:, 5, 0:n, 0:1], rt[:, 4, 0:n, 0:1]).then_inc(norm_chain, 1)
                dve.wait_ge(norm_chain, 2 * g + 2)
                wait(dve, cwb_mm, NE * (g - 1))
                nc.vector.scalar_tensor_tensor(out=cw[:, p, 0:n], in0=w, scalar=ROUTED_SCALE,
                                               in1=rt[:, 5, 0:n, 0:1].broadcast_to([128, n, NE]),
                                               op0=ALU.mult, op1=ALU.mult).then_inc(cw_ready, 1)

            def ffn(g, p, k, nxt):
                n = tiles_of(g)
                for j in range(NE):
                    dve.wait_ge(cwb_mm, g * NE + j + 1)
                    dve.wait_ge(relu_ready, g * NJ + SHARED // HID + j + 1)
                    wait(dve, sq_ready, g * NJ + SHARED // HID + j - 1)
                    nc.vector.tensor_tensor(gated[:, j % 2, 0:n * 128], relu[:, j % 2, 0:n * 128],
                                            psum[:, CWB_BANK[j % 2], 0:n * 128], ALU.mult).then_inc(gated_ready, 1)
                    if j == 1:
                        nxt("norm")
                dve.wait_ge(down_mm, (g + 1) * NJ)
                for t in range(0, n, 2):
                    m = min(2, n - t)
                    ins = nc.vector.scalar_tensor_tensor(
                        out=y[:, p, t:t + m].rearrange("p t e -> p (t e)"), in0=psum[:, DOWN_BANK + t // 2, 0:m * E],
                        scalar=g_tanh[:, 1:2], in1=xin2[:, p, t:t + m].rearrange("p t e -> p (t e)"),
                        op0=ALU.mult, op1=ALU.add)
                ins.then_inc(y_ready, 1)
                nxt("route")

            phase2(dve, ln, ffn)

        @block.tensor
        def _(pe):
            mm = nc.tensor.matmul
            pe.wait_ge(consts, N_CONST)
            pe.wait_ge(made, 4)

            pe.wait_ge(fills, 3)

            def row_scores(b, h):
                wait(pe, max_ready, H * b.n + h - 1)
                if h == 0:
                    pe.wait_ge(qs_in[b.buf], (b.round + 1) * (6 * 16))
                    pe.wait_ge(ks_in[b.buf], (b.round + 1) * (3 * 16))
                mm(psum[0:SQ, ROW_BANK[h % 2], 0:SK], qs[0:ROWS, b.buf, h], ks[0:ROWS, b.buf, h],
                   start=True, stop=True).then_inc(row_mm, 1)

            def static(*values):
                return all(isinstance(v, int) for v in values)

            def k_proj(b, half):
                if half == 0:
                    pe.wait_ge(ctx_in[b.buf], (b.round + 1) * 16)
                    wait(pe, mrow_ready, upto(1, b.n - 2))
                    if static(b.n) and b.n <= 2:
                        wait(pe, k_ready, 2 * b.n - 1)
                else:
                    wait(pe, v_ready, upto(NT, b.n - 2, 2))
                    if static(b.n) and b.n <= 1:
                        wait(pe, k_ready, 2 * b.n)
                for c in range(CI):
                    ins = mm(psum[:, (D0, D1)[half], 0:SK], wk_s[:, c, half * 128:(half + 1) * 128], ctxt[:, b.buf, c],
                             start=(c == 0), stop=(c == CI - 1))
                ins.then_inc(k_mm, 1)

            def x_transpose(b):
                pe.wait_ge(xn_ready, b.n + 1)
                wait(pe, att0_ready, b.n - 3)
                if static(b.n) and b.n <= 3:
                    wait(pe, v_ready, NT * (b.n - 1))
                    wait(pe, q_ready, b.n)
                for c in range(CI):
                    ins = nc.tensor.transpose(psum[:, D2, c * SQ:(c + 1) * SQ], xn[:, c * 128:(c + 1) * 128], ident[0:SQ, 0:SQ])
                ins.then_inc(xnt_mm, 1)

            def q_proj(b):
                pe.wait_ge(xnt_ready, b.n + 1)
                for half in range(2):
                    for c in range(CI):
                        ins = mm(psum[:, D2, half * SQ:(half + 1) * SQ], wq_s[:, c, half * 128:(half + 1) * 128],
                                 xnt[:, c], start=(c == 0), stop=(c == CI - 1))
                ins.then_inc(q_mm, 1)

            def v_proj(b, t):
                if t == 0:
                    wait(pe, q_ready, upto(1, b.n + 2))
                    if static(b.n) and b.n + 1 >= B:
                        pe.wait_ge(att0_ready, b.n - 2)
                elif t == 1:
                    wait(pe, x2_ready, b.n - 2)
                    if static(b.n) and b.n <= 2:
                        pe.wait_ge(k_ready, 2 * b.n + 4)
                else:
                    pe.wait_ge(v_ready, NT * b.n + 1)
                for c in range(CI):
                    ins = mm(psum[0:KT, (D2, D1, D2)[t], 0:E], ctxt[:, b.buf, c, t * KSTEP:t * KSTEP + KT], wv_s[:, c],
                             start=(c == 0), stop=(c == CI - 1))
                ins.then_inc(v_mm, 1)

            def scores(b, u):
                wait(pe, exp_ready, UNITS * b.n + u - 1)
                if u == 0:
                    pe.wait_ge(m_in[b.buf], (b.round + 1) * 32)
                c, t = unit(u)
                for j in range(HPU):
                    h = c * HPU + j
                    ins = mm(psum[0:KT, SCORE_BANK[u % 2], j * SQ:(j + 1) * SQ], ks[0:MROWS, b.buf, h, t * KSTEP:t * KSTEP + KT],
                             qs[0:MROWS, b.buf, h], start=True, stop=True)
                ins.then_inc(score_mm, 1)

            def times_v(b, u):
                pe.wait_ge(exp_ready, UNITS * b.n + u + 1)
                if u == 0:
                    pe.wait_ge(v_ready, NT * (b.n + 1))
                    wait(pe, pvt_ready, b.n)
                c, t = unit(u)
                n = KT if t == NT - 1 else KSTEP
                for j in range(HPU):
                    ins = mm(psum[j * DV:(j + 1) * DV, PV_BANK, c * SQ:(c + 1) * SQ], vs[0:n, b.buf, t, c * HPU + j],
                             probs[0:n, u, j * SQ:(j + 1) * SQ], start=(t == 0), stop=(t == NT - 1))
                ins.then_inc(pv_mm, 1)

            def pv_transpose(b):
                pe.wait_ge(pvt_ready, b.n + 1)
                wait(pe, v_ready, upto(NT, b.n + 3))
                if static(b.n) and b.n + 2 >= B:
                    pe.wait_ge(att0_ready, b.n)
                for c in range(H // HPU):
                    ins = nc.tensor.transpose(psum[0:SQ, D2, c * 128:(c + 1) * 128], pvt[:, c * SQ:(c + 1) * SQ], ident[:])
                ins.then_inc(pvt_mm, 1)

            def att_transpose(b):
                pe.wait_ge(att_ready, b.n + 1)
                wait(pe, k_ready, upto(2, b.n + 4, 1))
                if static(b.n) and b.n + 4 >= B:
                    pe.wait_ge(mrow_ready, upto(1, b.n + 2))
                for c in range(CI):
                    ins = nc.tensor.transpose(psum[:, D0, c * SQ:(c + 1) * SQ], att[:, c * 128:(c + 1) * 128], ident[0:SQ, 0:SQ])
                ins.then_inc(att_t_mm, 1)

            def out_proj(b):
                pe.wait_ge(att_t_ready, b.n + 1)
                wait(pe, k_ready, upto(2, b.n + 4, 2))
                if static(b.n) and b.n + 4 >= B:
                    pe.wait_ge(v_ready, upto(NT, b.n + 2, 2))
                for c in range(CI):
                    ins = mm(psum[0:SQ, D1, 0:E], att_t[:, c], wo_s[:, c], start=(c == 0), stop=(c == CI - 1))
                ins.then_inc(o_mm, 1)

            def max_transpose(b):
                pe.wait_ge(max_ready, H * (b.n + 1))
                wait(pe, att_t_ready, b.n - 1)
                if static(b.n) and (b.n <= 1 or b.n + 2 >= B):
                    pe.wait_ge(k_ready, upto(2, b.n + 2, 1))
                nc.tensor.transpose(psum[0:H, D0, 0:SQ], negmax[:], ident[0:SQ, 0:SQ]).then_inc(mt_mm, 1)

            def step(bl, bv, bm, be, bf):
                for i in range(H):
                    if bm is not None:
                        row_scores(bm, i)
                    if bl is not None and i < 2:
                        k_proj(bl, i)
                    if bf is not None and i == 2:
                        pv_transpose(bf)
                    if be is not None and 2 <= i < 2 + UNITS:
                        scores(be, i - 2)
                    if bl is not None and i == 4:
                        x_transpose(bl)
                    if bf is not None and i == 6:
                        att_transpose(bf)
                    if bl is not None and i == 7:
                        q_proj(bl)
                    if bf is not None and i == 9:
                        out_proj(bf)
                    if be is not None and 4 <= i < 4 + UNITS:
                        times_v(be, i - 4)
                if bv is not None:
                    v_proj(bv, 0)
                if bm is not None:
                    max_transpose(bm)
                if bv is not None:
                    v_proj(bv, 1)
                    v_proj(bv, 2)

            phase1(pe, step)
            pe.wait_ge(x2_ready, B)
            pe.wait_ge(att0_ready, B)
            pe.wait_ge(mrow_ready, B)

            def ln(g, p, k, part):
                n = tiles_of(g)
                if part in range(n):
                    t = part
                    pe.wait_ge(t_xn, g * GT + t + 1)
                    wait(pe, t_xnt, g * GT + t)
                    for c in range(CI):
                        ins = nc.tensor.transpose(psum[:, LN_BANK, c * 128:(c + 1) * 128],
                                                  xn2[:, p, t, c * 128:(c + 1) * 128], ident[:])
                    ins.then_inc(t_xnt_mm, 1)
                if part != "route":
                    return
                pe.wait_ge(t_xnt, g * GT + n)
                wait(pe, esig_ready, g)
                for t in range(n):
                    for c in range(CI):
                        ins = mm(psum[:, LOGIT_BANK, t * NE:(t + 1) * NE], xnt2[:, p, c, t * 128:(t + 1) * 128], gate_s[:, c],
                                 start=(c == 0), stop=(c == CI - 1))
                ins.then_inc(logit_mm, 1)

            def up(g, p, j):
                wait(pe, relu_ready, g * NJ + j - 1)
                n = tiles_of(g) * 128
                for c in range(CI):
                    ins = mm(psum[:, UP_BANK[j % 2], 0:n], up_s[:, c, j * HID:(j + 1) * HID], xnt2[:, p, c, 0:n],
                             start=(c == 0), stop=(c == CI - 1))
                ins.then_inc(up_mm, 1)

            def spread_weights(g, p, j):
                if j == 0:
                    pe.wait_ge(cw_ready, g + 1)
                wait(pe, gated_ready, g * NE + j - 1)
                for t in range(tiles_of(g)):
                    ins = nc.tensor.transpose(psum[:, CWB_BANK[j % 2], t * 128:(t + 1) * 128],
                                              cw[:, p, t, j:j + 1].broadcast_to([128, 128]), ident[:])
                ins.then_inc(cwb_mm, 1)

            def down(g, p, j):
                pe.wait_ge(sq_ready, g * NJ + j + 1)
                if j == 0:
                    wait(pe, y_ready, g)
                for t in range(tiles_of(g)):
                    ins = mm(psum[:, DOWN_BANK + t // 2, (t % 2) * E:(t % 2 + 1) * E], sq[:, j % 2, t * 128:(t + 1) * 128],
                             down_s[:, j], start=(j == 0 and t % 2 == 0), stop=(j == NJ - 1), skip_group_check=True)
                ins.then_inc(down_mm, 1)

            def ffn(g, p, k, nxt):
                for j in range(NJ + 1):
                    if j < NJ:
                        up(g, p, j)
                        if j >= SHARED // HID:
                            spread_weights(g, p, j - SHARED // HID)
                    if j >= 1:
                        down(g, p, j - 1)
                    if j >= 8:
                        nxt(j - 8 if j < NJ else "route")

            phase2(pe, ln, ffn)


_ORDER = ("x", "ctx_t", "g_x", "g_f", "wq", "bq", "wk", "bk", "wv", "bv", "wo", "bo",
          "gate_t", "gate_b", "up_t", "down_t", "sup_t", "sdown_t")


def kernel(**inputs):
    import numpy as np
    import concourse.bacc as bacc
    from concourse.bass_utils import run_bass_kernel_spmd as run

    i = {k: np.asarray(v) for k, v in inputs.items()}

    def by_dim(w):
        return w.reshape(w.shape[:-1] + (H, D)).swapaxes(-1, -2).reshape(w.shape)

    laid = {
        "x": i["x"].reshape(TOK, E),
        "ctx_t": i["ctx_1024"].transpose(0, 2, 1),
        "g_x": i["g_xattn"], "g_f": i["g_ffn"],
        "wq": by_dim(i["L0_xattn_Wq"]), "bq": by_dim(i["L0_xattn_bq"]),
        "wk": by_dim(i["L0_xattn_Wk"]), "bk": by_dim(i["L0_xattn_bk"]),
        "wv": i["L0_xattn_Wv"], "bv": i["L0_xattn_bv"], "wo": i["L0_xattn_Wo"], "bo": i["L0_xattn_bo"],
        "gate_t": i["L0_ffn_gate_weight"].T, "gate_b": i["L0_ffn_gate_bias"],
        "up_t": i["L0_ffn_up_weights"].reshape(NE * HID, E).T,
        "down_t": i["L0_ffn_down_weights"].transpose(0, 2, 1).reshape(NE * HID, E),
        "sup_t": i["L0_ffn_shared_up_weight"].T, "sdown_t": i["L0_ffn_shared_down_weight"].T,
    }
    nc = bacc.Bacc("TRN2", target_bir_lowering=False, num_devices=1)
    arrays, args = {}, []
    for name in _ORDER:
        a = np.ascontiguousarray(laid[name])
        arrays[f"in_{name}"] = a
        args.append(nc.dram_tensor(f"in_{name}", a.shape, mybir.dt.from_np(a.dtype), kind="ExternalInput").ap())
    args.append(nc.dram_tensor("out_0", (TOK, E), F32, kind="ExternalOutput").ap())
    build(nc, *args)
    r = run(nc, [arrays], core_ids=[0])
    return r.results[0]["out_0"].reshape(B, SQ, E)
```

```python
from contextlib import ExitStack

import concourse.bass as bass
from concourse import mybir

F32 = mybir.dt.float32
BF16 = mybir.dt.bfloat16
F32R = mybir.dt.float32r
ALU = mybir.AluOpType
ACT = mybir.ActivationFunctionType
AX_X = mybir.AxisListType.X

B, SQ, SK, E = 32, 100, 361, 256
SKP = SK + 1
H, D = 16, 16
CI = E // 128
TOK = B * SQ
NE, HID, SHARED = 8, 128, 512
NJ = NE + SHARED // HID
EPS = 1e-5
SCALE = float(D) ** -0.5
ROUTED_SCALE = 2.5
K_PARTS = (0, 1, 2, 0, 1, 0)
Q_PARTS = (0, 0, 0, 1, 1, 2)
ROWS = 6 * D
MROWS = ROWS + 2
KT = 121
KSTEP = 120
NT = 3
HPU = 4
UNITS = H // HPU * NT
DV = 2 * D
GT = 4
TILES = TOK // 128
GROUPS = -(-TILES // GT)
SETS = NE + 1
LN_STATS, LN_NORM, LN_T = 3, 4, 5
K_AT, X_AT, Q_AT, SUM_AT, DIV_AT, ATT_AT, OUT_AT, KR_AT = (0, 3), 5, 7, 2, 3, 6, 8, 7
SPLIT_AT = 14
FIRST_LN_AT = 12
ROUTER_OPS = 19


def unit(u):
    return u // NT, u % NT


def upto(per, b, extra=0):
    n = per * b + extra
    return min(n, per * B) if isinstance(n, int) else n


def static(*values):
    return all(isinstance(v, int) for v in values)


def wait(eng, sem, value):
    if not (isinstance(value, int) and value <= 0):
        eng.wait_ge(sem, value)


def at_start(b):
    return isinstance(b.n, int) and b.n == 0


def at_end(b):
    return isinstance(b.n, int) and b.n == B - 1


class At:

    def __init__(self, k, c):
        self.k, self.c = k, c
        self.buf = c % 3
        self.round = k + c // 3
        self.n = k * 3 + c

    def __add__(self, d):
        return At(self.k, self.c + d)


def build(nc, x, ctx_t, g_x, g_f, wq, bq, wk, bk, wv, bv, wo, bo, gate_t, gate_b, up_t, down_t, sup_t, sdown_t, out):
    kscr = nc.dram_tensor("kscr", [B, 3, E, SK], BF16, kind="Internal").ap()
    qscr = nc.dram_tensor("qscr", [B, 3, E, SQ], BF16, kind="Internal").ap()
    x2scr = nc.dram_tensor("x2scr", [TOK, E], F32, kind="Internal").ap()

    with ExitStack() as ctx:
        def sb(name, shape, dt=F32):
            return ctx.enter_context(nc.sbuf_tensor(name, shape, dt))

        def sem(name):
            return ctx.enter_context(nc.semaphore(name))

        psum = ctx.enter_context(nc.psum_tensor("psum", [128, 8, 512], F32))

        ident = sb("ident", [128, 128])
        wq_s, wo_s = (sb(n, [128, CI, E]) for n in ("wq_s", "wo_s"))
        wk_hi, wk_lo, wv_hi, wv_lo = (sb(n, [128, CI, E], F32R) for n in ("wk_hi", "wk_lo", "wv_hi", "wv_lo"))
        bq_s, bk_s = sb("bq_s", [128, 2]), sb("bk_s", [128, 2])
        bv_s, bo_s, gbo = sb("bv_s", [SQ, E]), sb("bo_s", [SQ, E]), sb("gbo", [SQ, E])
        up_s = sb("up_s", [128, CI, NJ * HID])
        down_s = sb("down_s", [128, NJ, E])
        gate_s = sb("gate_s", [128, CI, NE])
        gb_s = sb("gb_s", [128, NE])
        lower = sb("lower", [128, NE, NE])
        g_raw, g_tanh = sb("g_raw", [128, 2]), sb("g_tanh", [128, 2])
        half_neg = sb("half_neg", [128, GT])
        eps_s = sb("eps_s", [128, GT])

        xl = sb("xl", [SQ, 3, E])
        stats = sb("stats", [SQ, 3, 6])
        carrier = sb("carrier", [128, 1])
        meanvar = sb("meanvar", [SQ, 3, 2])
        vareps, rstd = sb("vareps", [SQ, 3]), sb("rstd", [SQ, 3])
        xn = sb("xn", [SQ, E])
        xnt = sb("xnt", [128, CI, SQ])
        qf, qr = sb("qf", [128, 2, SQ]), sb("qr", [128, 2, SQ])
        qp = sb("qp", [128, 3, 3, 2, SQ], BF16)
        qs = sb("qs", [128, 3, H, SQ], BF16)
        negmax = sb("negmax", [SQ, H])
        mrow = sb("mrow", [H, 2, SQ], BF16)
        probs = sb("probs", [128, UNITS, HPU * SQ])
        pvt = sb("pvt", [128, HPU * SQ])
        rden = sb("rden", [SQ, H])
        att0, att = sb("att0", [SQ, E]), sb("att", [SQ, E])
        att_t = sb("att_t", [128, CI, SQ])
        xr = sb("xr", [SQ, 3, E])
        xb = sb("xb", [SQ, 3, E])
        x2 = sb("x2", [SQ, 3, E])

        xin_even = sb("xin_even", [128, GT, E])
        xn2 = sb("xn2", [128, GT, E])
        xraw = sb("xraw", [128, CI, GT * 128])
        xhi_even, xlo_even = (sb(n, [128, CI, GT * 128], F32R) for n in ("xhi_even", "xlo_even"))
        stats2 = sb("stats2", [128, 2, GT, 6])
        meanvar2 = sb("meanvar2", [128, 2, GT, 2])
        vareps2, rstd2 = sb("vareps2", [128, 2, GT]), sb("rstd2", [128, 2, GT])
        spare = probs[:].rearrange("p u n -> p (u n)")
        n_y, n_h = 2 * GT * E, GT * 128
        y = spare[:, 0:n_y].rearrange("p (a t e) -> p a t e", a=2, t=GT)
        relu = spare[:, n_y:n_y + 2 * n_h].rearrange("p (a n) -> p a n", a=2)
        wk_raw, wv_raw = (spare[:, i * CI * E:(i + 1) * CI * E].rearrange("p (c n) -> p c n", c=CI) for i in range(2))

        with ExitStack() as early:
            def sb1(name, shape, dt=F32):
                return early.enter_context(nc.sbuf_tensor(name, shape, dt))

            kp = sb1("kp", [128, 3, 3, 2, SK], BF16)
            ctx_raw = sb1("ctx_raw", [128, CI, SK])
            ctx_hi, ctx_lo = (sb1(n, [128, 3, CI, SKP], F32R) for n in ("ctx_hi", "ctx_lo"))
            kf, kr = sb1("kf", [128, 2, SK]), sb1("kr", [128, 2, SK])
            ks_buf = {i: sb1(f"ks{i}", [128, H, SK], BF16) for i in (2, 0, 1)}
            ks = [ks_buf[i] for i in range(3)]
            vs = sb1("vs", [128, 3, NT, H, DV])
        up_hi, down_hi = sb("up_hi", [128, CI, NJ * HID], F32R), sb("down_hi", [128, NJ, E], F32R)
        up_lo, down_lo = sb("up_lo", [128, CI, NJ * HID], F32R), sb("down_lo", [128, NJ, E], F32R)
        sq_hi, sq_lo = sb("sq_hi", [128, 3, GT * 128], F32R), sb("sq_lo", [128, 3, GT * 128], F32R)
        xin2 = [xin_even, sb("xin_odd", [128, GT, E])]
        xhi, xlo = [xhi_even, sb("xhi_odd", [128, CI, GT * 128], F32R)], [xlo_even, sb("xlo_odd", [128, CI, GT * 128], F32R)]
        sq = sb("sq", [128, 2, GT * 128])

        cw = sb("cw", [128, 2, GT, NE])
        rt = sb("rt", [128, 12, GT, NE])
        big = sb("big", [128, 2, GT, NE, NE])

        weights_in = sem("weights_in")
        consts = sem("consts")
        ffn_weights_in = sem("ffn_weights_in")
        ones_in = sem("ones_in")
        made = sem("made")
        fills = sem("fills")
        gates_ready = sem("gates_ready")
        gbo_ready = sem("gbo_ready")
        xl_in = [sem(f"xl_in{i}") for i in range(3)]
        stats_done, meanvar_ready, vareps_ready = sem("stats_done"), sem("meanvar_ready"), sem("vareps_ready")
        rstd_ready, xn_ready = sem("rstd_ready"), sem("xn_ready")
        xnt_mm, xnt_ready = sem("xnt_mm"), sem("xnt_ready")
        q_mm, q_ready, q_chain, qp_ready = sem("q_mm"), sem("q_ready"), sem("q_chain"), sem("qp_ready")
        qscr_out = [sem(f"qscr_out{i}") for i in range(3)]

        ctx_in, ctx_hi_ready, ctx_ready = sem("ctx_in"), sem("ctx_hi_ready"), sem("ctx_ready")
        wkv_hi_ready, wkv_lo_ready = sem("wkv_hi_ready"), sem("wkv_lo_ready")
        xr_in = [sem(f"xr_in{i}") for i in range(3)]
        qs_in = [sem(f"qs_in{i}") for i in range(3)]
        ks_in = [sem(f"ks_in{i}") for i in range(3)]
        m_in = [sem(f"m_in{i}") for i in range(3)]
        kscr_out = [sem(f"kscr_out{i}") for i in range(3)]
        x2_out = [sem(f"x2_out{i}") for i in range(3)]
        k_mm, k_ready, kr_ready, k_chain, kp_ready = (
            sem("k_mm"), sem("k_ready"), sem("kr_ready"), sem("k_chain"), sem("kp_ready"))
        v_mm, v_ready = sem("v_mm"), sem("v_ready")
        row_mm, max_ready, mt_mm, mhi_ready, mrow_ready = (
            sem("row_mm"), sem("max_ready"), sem("mt_mm"), sem("mhi_ready"), sem("mrow_ready"))
        score_mm, exp_ready, pv_mm = sem("score_mm"), sem("exp_ready"), sem("pv_mm")
        pvt_ready, pvt_mm = sem("pvt_ready"), sem("pvt_mm")
        rden_ready, att0_ready, att_ready = sem("rden_ready"), sem("att0_ready"), sem("att_ready")
        att_t_mm, att_t_ready, o_mm, xb_ready, x2_ready = (
            sem("att_t_mm"), sem("att_t_ready"), sem("o_mm"), sem("xb_ready"), sem("x2_ready"))

        ln_in = [sem(f"ln_in{i}") for i in range(2)]
        t_stats, t_meanvar, t_vareps, t_rstd, t_xn = (
            sem("t_stats"), sem("t_meanvar"), sem("t_vareps"), sem("t_rstd"), sem("t_xn"))
        t_xnt_mm, t_xhi, t_xlo = sem("t_xnt_mm"), sem("t_xhi"), sem("t_xlo")
        weights_hi, lo_weights = sem("weights_hi"), sem("lo_weights")
        logit_mm, esig_ready, router, cw_ready = sem("logit_mm"), sem("esig_ready"), sem("router"), sem("cw_ready")
        up_mm, relu_ready, hi_ready, lo_ready, down_mm = (
            sem("up_mm"), sem("relu_ready"), sem("hi_ready"), sem("lo_ready"), sem("down_mm"))
        norm_chain = sem("norm_chain")
        acc_ready = sem("acc_ready")
        y_out = [sem(f"y_out{i}") for i in range(2)]

        N_WEIGHTS, N_CONST, N_FFN = 6 * 16, 8 * 16, 4 * 16

        ROW_BANK, SCORE_BANK, PV_BANK, D0, D1, D2 = (0, 1), (2, 3), 4, 5, 6, 7
        LN_BANK, LOGIT_BANK, UP_BANK, DOWN_BANK = 0, 1, (2, 3), (4, 6)

        def phase1(eng, do, before={}):
            def edge(s):
                before.get(s, lambda: None)()
                do(*(At((s + d) // 3, (s + d) % 3) if 0 <= s + d < B else None for d in (3, 2, 1, 0, -1)))

            loops = (B - 4) // 3 + 1
            for s in range(-3, 3):
                edge(s)
            with eng.Fori(1, loops - 1) as k:
                for c in range(3):
                    do(*(At(k, c + d) for d in (3, 2, 1, 0, -1)))
            for s in range(3 * (loops - 1), B + 1):
                edge(s)

        def first_of(g):
            return (0, 2)[g] if isinstance(g, int) and g < 2 else g * GT - 3

        def tiles_of(g):
            return g + 2 if isinstance(g, int) and g < 2 else GT

        def phase2(eng, ffn):
            ffn((0, 0, 0), (1, 1, 0))
            ffn((1, 1, 0), (2, 0, 1))
            with eng.Fori(0, 2) as k:
                ffn((k * 2 + 2, 0, k + 1), (k * 2 + 3, 1, k + 1))
                ffn((k * 2 + 3, 1, k + 1), (k * 2 + 4, 0, k + 2))
            ffn((6, 0, 3), None)

        FIRST_SLOTS = {3: 0, 7: 1}

        def slots_left(g):
            return range(len(FIRST_SLOTS) if isinstance(g, int) and g == 0 else 0, NJ)

        WEIGHTS = tuple(tuple(t[:].rearrange("p a b -> p (a b)") for t in ts)
                        for ts in ((up_s, up_hi, up_lo), (down_s, down_hi, down_lo)))
        PART = NJ * E // 4

        block = ctx.enter_context(nc.Block())

        @block.sync
        def _(sp):
            def load_consts():
                sp.dma_start(wv_raw, wv.rearrange("(c p) n -> p c n", p=128)).then_inc(consts, 16)
                for n, g in enumerate((g_x, g_f)):
                    sp.dma_start(g_raw[:, n:n + 1], g.partition_broadcast(128)).then_inc(consts, 16)
                for dst, src in (
                    (wo_s, wo.rearrange("(c p) n -> p c n", p=128)),
                    (bv_s, bv.partition_broadcast(SQ)), (bo_s, bo.partition_broadcast(SQ)),
                    (gb_s, gate_b.partition_broadcast(128)),
                    (gate_s, gate_t.rearrange("(c p) n -> p c n", p=128)),
                ):
                    sp.dma_start(dst[:], src).then_inc(consts, 16)

            def load_ffn_weights():
                for dst, src, n in (
                    (up_s[:, :, 0:SHARED], sup_t, 128), (up_s[:, :, SHARED:], up_t, 128),
                    (down_s[:, 0:SHARED // HID, :], sdown_t, HID), (down_s[:, SHARED // HID:, :], down_t, HID),
                ):
                    sp.dma_start(dst, src.rearrange("(c p) n -> p c n", p=n)).then_inc(ffn_weights_in, 16)

            def load_ahead(b):
                wait(sp, ctx_ready, b.n)
                sp.dma_start(ctx_raw[:], ctx_t[b.n].rearrange("(c p) n -> p c n", p=128)).then_inc(ctx_in, 16)
                wait(sp, xn_ready, b.n - 2)
                sp.dma_start(xl[:, b.buf], x[bass.ds(b.n * SQ, SQ), :]).then_inc(xl_in[b.buf], 16)

            def step(bl, bv, bm, be, bf):
                if bl is not None and not at_end(bl):
                    load_ahead(bl + 1)
                if bv is not None:
                    wait(sp, score_mm, UNITS * (bv.n - 2))
                    sp.wait_ge(kscr_out[bv.buf], (bv.round + 1) * 16)
                    kv = kscr[bv.n].rearrange("r (d h) k -> (r d) (h k)", h=H)
                    for lo, n in ((0, 3), (3, 2), (5, 1)):
                        sp.dma_start(ks[bv.buf][lo * D:(lo + n) * D], kv[0:n * D].rearrange("p (h k) -> p h k", h=H)).then_inc(ks_in[bv.buf], 16)
                    sp.wait_ge(qscr_out[bv.buf], (bv.round + 1) * 16)
                    for r in range(6):
                        sp.dma_start(qs[r * D:(r + 1) * D, bv.buf],
                                     qscr[bv.n, Q_PARTS[r]].rearrange("(d h) q -> d h q", h=H)).then_inc(qs_in[bv.buf], 16)
                if bm is not None:
                    wait(sp, xb_ready, bm.n - 2)
                    sp.dma_start(xr[:, bm.buf], x[bass.ds(bm.n * SQ, SQ), :]).then_inc(xr_in[bm.buf], 16)
                if bl is not None:
                    sp.wait_ge(kp_ready, bl.n + 1)
                    sp.dma_start(kscr[bl.n].rearrange("r (a p) k -> p r a k", p=128), kp[:, bl.buf]).then_inc(kscr_out[bl.buf], 16)
                    sp.wait_ge(qp_ready, bl.n + 1)
                    sp.dma_start(qscr[bl.n].rearrange("r (a p) q -> p r a q", p=128), qp[:, bl.buf]).then_inc(qscr_out[bl.buf], 16)
                if bf is not None:
                    sp.wait_ge(x2_ready, bf.n + 1)
                    sp.dma_start(x2scr[bass.ds(bf.n * SQ, SQ), :], x2[:, bf.buf]).then_inc(x2_out[bf.buf], 16)
                if bm is not None:
                    sp.wait_ge(mrow_ready, bm.n + 1)
                    for r in range(2):
                        sp.dma_start(qs[ROWS + r:ROWS + r + 1, bm.buf], mrow[:, r, :]).then_inc(m_in[bm.buf], 16)

            x2_v = x2scr[first_of(2) * 128:TOK, :].rearrange("(g t p) e -> g p t e", t=GT, p=128)
            out_v = out[first_of(2) * 128:TOK, :].rearrange("(g t p) e -> g p t e", t=GT, p=128)

            def group_of(v, whole, g):
                if isinstance(g, int) and g < 2:
                    return whole[first_of(g) * 128:(first_of(g) + tiles_of(g)) * 128, :].rearrange("(t p) e -> p t e", p=128)
                return v[g - 2]

            def load_group(g, p, k):
                sp.dma_start(xin2[p][:, 0:tiles_of(g)], group_of(x2_v, x2scr, g)).then_inc(ln_in[p], 16)

            def load_first():
                for i in range(3):
                    sp.wait_ge(x2_out[i], 16 * len(range(i, -(-tiles_of(0) * 128 // SQ), 3)))
                load_group(0, 0, 0)

            def load_second():
                for i in range(3):
                    sp.wait_ge(x2_out[i], 16 * len(range(i, -(-first_of(2) * 128 // SQ), 3)))
                sp.wait_ge(score_mm, UNITS * B)
                load_group(1, 1, 0)

            def ffn(now, ahead):
                g, p, k = now
                if ahead and not (static(g) and g == 0):
                    load_group(*ahead)
                sp.wait_ge(acc_ready, (g + 1) * SETS)
                sp.dma_start(group_of(out_v, out, g), y[:, p, 0:tiles_of(g)]).then_inc(y_out[p], 16)

            load_ahead(At(0, 0))
            for dst, src in ((wk_raw, wk), (wq_s[:], wq)):
                sp.dma_start(dst, src.rearrange("(c p) n -> p c n", p=128)).then_inc(weights_in, 16)
            for half in range(2):
                for dst, src in ((bk_s, bk), (bq_s, bq)):
                    sp.dma_start(dst[:, half:half + 1], src.rearrange("(a p o) -> a p o", p=128, o=1)[half]).then_inc(weights_in, 16)
            load_consts()
            sp.wait_ge(made, 5)
            for i in (1, 2):
                sp.dma_start(ks[i][ROWS:MROWS], ks[0][ROWS:MROWS]).then_inc(ones_in, 16)
            phase1(sp, step, {1: load_ffn_weights, B - 3: load_first, B: load_second})
            for i in range(3):
                sp.wait_ge(x2_out[i], 16 * len(range(i, B, 3)))
            phase2(sp, ffn)
            for p in range(2):
                sp.wait_ge(y_out[p], 16 * len(range(p, GROUPS, 2)))

        @block.gpsimd
        def _(gp):
            nc.gpsimd.memset(ident[:], 0.0).then_inc(made, 1)
            nc.gpsimd.memset(lower[:], 1.0).then_inc(made, 1)
            gp.wait_ge(made, 2)
            nc.gpsimd.affine_select(out=ident[:], in_=ident[:], compare_op=ALU.not_equal, fill=1.0, base=0,
                                    pattern=[[-1, 128]], channel_multiplier=1).then_inc(made, 1)
            nc.gpsimd.affine_select(out=lower[:], in_=lower[:], compare_op=ALU.is_gt, fill=0.0, base=0,
                                    pattern=[[1, NE], [-1, NE]], channel_multiplier=0).then_inc(made, 1)

            def make_rstd(mv, ve, rs, rows, n, inp, mid, outp, count):
                gp.wait_ge(inp, count)
                nc.gpsimd.tensor_tensor(ve, mv, eps_s[0:rows, 0:n], ALU.add).then_inc(mid, 1)
                gp.wait_ge(mid, count)
                nc.gpsimd.tensor_tensor(rs, ve, half_neg[0:rows, 0:n], ALU.pow).then_inc(outp, 1)

            gp.wait_ge(fills, 1)
            gp.wait_ge(made, 4)
            nc.gpsimd.memset(ks[0][ROWS:MROWS], 1.0).then_inc(made, 1)
            gp.wait_ge(made, 5)

            def context_lo(b):
                gp.wait_ge(ctx_hi_ready, b.n + 1)
                nc.gpsimd.tensor_tensor(ctx_lo[:, b.buf, :, 0:SK], ctx_raw[:], ctx_hi[:, b.buf, :, 0:SK],
                                        ALU.subtract).then_inc(ctx_ready, 1)

            def step(bl, bv, bm, be, bf):
                if bl is not None:
                    b = bl.buf
                    make_rstd(meanvar[:, b, 1:2], vareps[:, b:b + 1], rstd[:, b:b + 1], SQ, 1,
                              meanvar_ready, vareps_ready, rstd_ready, bl.n + 1)
                if bf is not None:
                    gp.wait_ge(att0_ready, bf.n + 1)
                    wait(gp, att_t_mm, bf.n)
                    nc.gpsimd.tensor_tensor(att[:], att0[:], bv_s[:], ALU.add).then_inc(att_ready, 1)
                if bl is not None and at_start(bl):
                    context_lo(bl + 1)
                if bl is not None:
                    gp.wait_ge(k_ready, 2 * bl.n + 2)
                    nc.gpsimd.tensor_tensor(kp[:, b, 1], kf[:], kp[:, b, 0], ALU.subtract).then_inc(k_chain, 1)
                    gp.wait_ge(kr_ready, bl.n + 1)
                    gp.wait_ge(k_chain, bl.n + 1)
                    nc.gpsimd.tensor_tensor(kp[:, b, 2], kr[:], kp[:, b, 1], ALU.subtract).then_inc(kp_ready, 1)
                    gp.wait_ge(q_ready, bl.n + 1)
                    nc.gpsimd.tensor_tensor(qp[:, b, 1], qf[:], qp[:, b, 0], ALU.subtract)
                    nc.gpsimd.tensor_tensor(qr[:], qf[:], qp[:, b, 0], ALU.subtract).then_inc(q_chain, 1)
                    gp.wait_ge(q_chain, bl.n + 1)
                    nc.gpsimd.tensor_tensor(qp[:, b, 2], qr[:], qp[:, b, 1], ALU.subtract).then_inc(qp_ready, 1)
                if bl is not None and not at_start(bl) and not at_end(bl):
                    context_lo(bl + 1)
                if be is not None:
                    gp.wait_ge(xr_in[be.buf], (be.round + 1) * 16)
                    wait(gp, x2_ready, be.n - 2)
                    wait(gp, x2_out[be.buf], be.round * 16)
                    nc.gpsimd.tensor_tensor(xb[:, be.buf], xr[:, be.buf], gbo[:], ALU.add).then_inc(xb_ready, 1)

            def ln(g, p, k, part):
                n = tiles_of(g)
                if part == "norm":
                    make_rstd(meanvar2[:, p, 0:n, 1], vareps2[:, p, 0:n], rstd2[:, p, 0:n], 128, n,
                              t_meanvar, t_vareps, t_rstd, g + 1)
                elif part in range(n):
                    at = slice(part * 128, (part + 1) * 128)
                    gp.wait_ge(t_xhi, first_of(g) + part + 1)
                    nc.gpsimd.tensor_tensor(xlo[p][:, :, at], xraw[:, :, at], xhi[p][:, :, at],
                                            ALU.subtract).then_inc(t_xlo, 1)

            def square_lo(g, p, k, j):
                n = tiles_of(g) * 128
                gp.wait_ge(hi_ready, g * NJ + j + 1)
                nc.gpsimd.tensor_tensor(sq_lo[:, j % 3, 0:n], sq[:, j % 2, 0:n], sq_hi[:, j % 3, 0:n],
                                        ALU.subtract).then_inc(lo_ready, 1)

            def ffn(now, ahead):
                for j in range(NJ):
                    if j + 2 < NJ:
                        square_lo(*now, j + 2)
                    elif ahead:
                        square_lo(*ahead, j + 2 - NJ)
                    if ahead and j == LN_STATS:
                        ln(*ahead, "norm")
                    if ahead and 0 <= j - LN_T < GT:
                        ln(*ahead, j - LN_T)

            phase1(gp, step, {0: lambda: gp.wait_ge(gbo_ready, 1),
                              B - 1: lambda: ln(0, 0, 0, "norm"),
                              B: lambda: [ln(0, 0, 0, t) for t in range(tiles_of(0))]})
            for j in range(2):
                square_lo(0, 0, 0, j)
            phase2(gp, ffn)

        @block.scalar
        def _(act):
            def context_hi(b):
                act.wait_ge(ctx_in, (b.n + 1) * 16)
                wait(act, v_mm, NT * (b.n - 2))
                nc.scalar.activation(ctx_hi[:, b.buf, :, 0:SK], ctx_raw[:], ACT.Copy).then_inc(ctx_hi_ready, 1)

            context_hi(At(0, 0))
            act.wait_ge(weights_in, N_WEIGHTS)
            nc.scalar.activation(wk_hi[:], wk_raw, ACT.Copy).then_inc(wkv_hi_ready, 1)

            def split_wv():
                act.wait_ge(consts, N_CONST)
                nc.scalar.activation(wv_hi[:], wv_raw, ACT.Copy).then_inc(wkv_hi_ready, 1)

            def make_gates():
                act.wait_ge(consts, N_CONST)
                nc.scalar.activation(g_tanh[:], g_raw[:], ACT.Tanh).then_inc(gates_ready, 1)

            def exp_unit(be, i):
                act.wait_ge(score_mm, UNITS * be.n + i + 1)
                wait(act, pv_mm, UNITS * (be.n - 1) + i + 1)
                nc.scalar.activation(probs[0:KT, i], psum[0:KT, SCORE_BANK[i % 2], 0:HPU * SQ], ACT.Exp,
                                     scale=SCALE).then_inc(exp_ready, 1)

            def split_first(full, part, bank, bias, done):
                nc.scalar.activation(full, bank, ACT.Identity, bias=bias)
                ins = nc.scalar.activation(part, bank, ACT.Identity, bias=bias)
                if done is not None:
                    ins.then_inc(done, 1)

            def step(bl, bv, bm, be, bf):
                for i in range(H):
                    if not (bl or bv or bm or be) and i in FIRST_SLOTS:
                        slot((0, 0, 0), (1, 1, 0), FIRST_SLOTS[i])
                    if be is not None and 2 <= i < 2 + UNITS:
                        exp_unit(be, i - 2)
                    if bl is not None and i in K_AT:
                        half = K_AT.index(i)
                        act.wait_ge(k_mm, 2 * bl.n + half + 1)
                        wait(act, kp_ready, bl.n)
                        wait(act, kscr_out[bl.buf], bl.round * 16)
                        split_first(kf[:, half], kp[:, bl.buf, 0, half], psum[:, (D0, D1)[half], 0:SK],
                                    bk_s[:, half:half + 1], k_ready)
                    if bl is not None and i == X_AT:
                        act.wait_ge(xnt_mm, bl.n + 1)
                        wait(act, q_mm, bl.n)
                        nc.scalar.activation(xnt[:], psum[:, D2, 0:CI * SQ].rearrange("p (c q) -> p c q", c=CI),
                                             ACT.Copy).then_inc(xnt_ready, 1)
                    if bf is not None and i == ATT_AT:
                        act.wait_ge(att_t_mm, bf.n + 1)
                        wait(act, o_mm, bf.n)
                        nc.scalar.activation(att_t[:], psum[:, D0, 0:CI * SQ].rearrange("p (c q) -> p c q", c=CI),
                                             ACT.Copy).then_inc(att_t_ready, 1)
                    if bl is not None and i == Q_AT:
                        act.wait_ge(q_mm, bl.n + 1)
                        wait(act, qp_ready, bl.n)
                        wait(act, qscr_out[bl.buf], bl.round * 16)
                        for half in range(2):
                            split_first(qf[:, half], qp[:, bl.buf, 0, half], psum[:, D2, half * SQ:(half + 1) * SQ],
                                        bq_s[:, half:half + 1], q_ready if half else None)
                    if bl is not None and i == (1 if at_start(bl) else SPLIT_AT) and not at_end(bl):
                        context_hi(bl + 1)
                    if be is not None and static(be.n) and be.n == B - 2 and i >= 4 and i % 2 == 0:
                        weights_hi_part(i // 2 - 2)
                    if be is not None and at_end(be) and i in (4, 6):
                        weights_hi_part(i // 2 + 4)
                    if be is not None and at_end(be) and i == FIRST_LN_AT:
                        for t in range(tiles_of(0)):
                            ln(0, 0, 0, t)
                if be is not None:
                    act.wait_ge(pv_mm, UNITS * (be.n + 1))
                    wait(act, pvt_mm, be.n)
                    nc.scalar.activation(pvt[:], psum[:, PV_BANK, 0:HPU * SQ], ACT.Copy).then_inc(pvt_ready, 1)
                if bv is not None:
                    for t in range(NT):
                        act.wait_ge(v_mm, NT * bv.n + t + 1)
                        wait(act, pv_mm, UNITS * (bv.n - 2))
                        nc.scalar.activation(vs[0:KT, bv.buf, t, :, 0:D],
                                             psum[0:KT, (D2, D1, D2)[t], 0:E].rearrange("p (h d) -> p h d", h=H),
                                             ACT.Copy).then_inc(v_ready, 1)

            def weights_hi_part(n):
                if n == 0:
                    for i in range(3):
                        act.wait_ge(kscr_out[i], 16 * len(range(i, B, 3)))
                    act.wait_ge(kp_ready, B)
                    act.wait_ge(v_mm, NT * B)
                    act.wait_ge(ffn_weights_in, N_FFN)
                (w, hi, _), at = WEIGHTS[n // 4], slice(n % 4 * PART, (n % 4 + 1) * PART)
                nc.scalar.activation(hi[:, at], w[:, at], ACT.Copy).then_inc(weights_hi, 1)

            def ln(g, p, k, part):
                n = tiles_of(g)
                if part in range(n):
                    at = slice(part * 128, (part + 1) * 128)
                    bank = psum[:, LN_BANK, 0:CI * 128].rearrange("p (c q) -> p c q", c=CI)
                    act.wait_ge(t_xnt_mm, first_of(g) + part + 1)
                    wait(act, logit_mm, g)
                    wait(act, t_xlo, first_of(g))
                    nc.scalar.activation(xraw[:, :, at], bank, ACT.Copy)
                    wait(act, up_mm, NJ * (g - 1))
                    nc.scalar.activation(xhi[p][:, :, at], bank, ACT.Copy).then_inc(t_xhi, 1)
                if part != "route":
                    return
                act.wait_ge(logit_mm, g + 1)
                wait(act, cw_ready, g)
                nc.scalar.activation(rt[:, 0, 0:n], psum[:, LOGIT_BANK, 0:n * NE].rearrange("p (t e) -> p t e", e=NE),
                                     ACT.Exp, scale=-1.0).then_inc(esig_ready, 1)

            def square_hi(g, p, k, j):
                n = tiles_of(g) * 128
                act.wait_ge(up_mm, g * NJ + j + 1)
                nc.scalar.activation(relu[:, j % 2, 0:n], psum[:, UP_BANK[j % 2], 0:n], ACT.Relu).then_inc(relu_ready, 1)
                act.wait_ge(relu_ready, g * NJ + j + 1)
                wait(act, lo_ready, g * NJ + j - 1)
                nc.scalar.activation(sq[:, j % 2, 0:n], relu[:, j % 2, 0:n], ACT.Square)
                wait(act, down_mm, g * NJ + j - 2)
                nc.scalar.activation(sq_hi[:, j % 3, 0:n], relu[:, j % 2, 0:n], ACT.Square).then_inc(hi_ready, 1)

            def slot(now, ahead, j):
                if j + 2 < NJ:
                    square_hi(*now, j + 2)
                elif ahead:
                    square_hi(*ahead, j + 2 - NJ)
                if ahead and 0 <= j - LN_T < GT:
                    ln(*ahead, j - LN_T)
                if ahead and j == LN_T + GT:
                    ln(*ahead, "route")

            def ffn(now, ahead):
                for j in slots_left(now[0]):
                    slot(now, ahead, j)

            phase1(act, step, {-2: split_wv, -1: make_gates,
                               B: lambda: (ln(0, 0, 0, "route"), square_hi(0, 0, 0, 0), square_hi(0, 0, 0, 1))})
            phase2(act, ffn)

        @block.vector
        def _(dve):
            nc.vector.memset(half_neg[:], -0.5)
            for parts in (ctx_hi, ctx_lo):
                nc.vector.memset(parts[:, :, :, SK:SKP].bitcast(F32), 0.0)
            nc.vector.memset(eps_s[:], EPS).then_inc(fills, 1)

            def fill_v_and_bias():
                nc.vector.memset(vs[:, :, :, :, D:DV], 1.0).then_inc(fills, 1)
                dve.wait_ge(consts, N_CONST)
                dve.wait_ge(gates_ready, 1)
                nc.vector.tensor_scalar(gbo[:], bo_s[:], g_tanh[0:SQ, 0:1], None, ALU.mult).then_inc(gbo_ready, 1)

            def aggregate(last, source, rows, seen, count):
                dve.wait_ge(seen, count)
                nc.vector.tensor_copy(carrier[0:rows], last)
                for out_ap, in_ap in source:
                    ins = nc.vector.bn_aggr(out_ap, in_ap)
                return ins

            def step(bl, bv, bm, be, bf):
                for h in range(H):
                    if bm is not None:
                        dve.wait_ge(row_mm, H * bm.n + h + 1)
                        if h == 0:
                            wait(dve, mt_mm, bm.n)
                        nc.vector.tensor_reduce(negmax[:, h:h + 1], psum[0:SQ, ROW_BANK[h % 2], 0:SK],
                                                axis=AX_X, op=ALU.max, negate=True).then_inc(max_ready, 1)
                    if bl is not None and h == 0:
                        b = bl.buf
                        dve.wait_ge(xl_in[b], (bl.round + 1) * 16)
                        nc.vector.bn_stats(stats[:, b], xl[:, b]).then_inc(stats_done, 1)
                        aggregate(stats[:, b, 0:1], [(meanvar[:, b], stats[:, b])], SQ, stats_done,
                                  bl.n + 1).then_inc(meanvar_ready, 1)
                    if bl is not None and h == 2:
                        dve.wait_ge(rstd_ready, bl.n + 1)
                        wait(dve, xnt_mm, bl.n)
                        nc.vector.tensor_scalar(xn[:], xl[:, b], meanvar[:, b, 0:1], rstd[:, b:b + 1],
                                                ALU.subtract, ALU.mult).then_inc(xn_ready, 1)
                    if bf is not None and h == DIV_AT:
                        pv = psum[0:SQ, D2, :].rearrange("p (h r) -> p h r", r=DV)
                        dve.wait_ge(pvt_mm, bf.n + 1)
                        nc.vector.reciprocal(rden[:], pv[:, :, D]).then_inc(rden_ready, 1)
                        dve.wait_ge(rden_ready, bf.n + 1)
                        wait(dve, att_ready, bf.n)
                        nc.vector.tensor_tensor(att0[:].rearrange("p (h d) -> p h d", h=H), pv[:, :, 0:D],
                                                rden[:].unsqueeze(2).broadcast_to([SQ, H, D]), ALU.mult).then_inc(att0_ready, 1)
                    if bl is not None and h == KR_AT:
                        dve.wait_ge(k_ready, 2 * bl.n + 2)
                        wait(dve, kp_ready, bl.n)
                        nc.vector.tensor_tensor(kr[:], kf[:], kp[:, b, 0], ALU.subtract).then_inc(kr_ready, 1)
                    if bf is not None and h == OUT_AT + 1:
                        dve.wait_ge(o_mm, bf.n + 1)
                        dve.wait_ge(xb_ready, bf.n + 1)
                        nc.vector.scalar_tensor_tensor(out=x2[:, bf.buf], in0=psum[0:SQ, D1, 0:E], scalar=g_tanh[0:SQ, 0:1],
                                                       in1=xb[:, bf.buf], op0=ALU.mult, op1=ALU.add).then_inc(x2_ready, 1)
                    if bf is not None and at_end(bf) and h == DIV_AT + 1:
                        ln(0, 0, 0, "route")
                    if be is not None and at_end(be):
                        if h == DIV_AT + 1:
                            ln(0, 0, 0, "norm")
                        if h == DIV_AT + 2:
                            ln(0, 0, 0, "normalise")
                        if h >= H - 8:
                            weights_lo_part(h - (H - 8))
                if bm is not None:
                    dve.wait_ge(mt_mm, bm.n + 1)
                    prev = bm + -1
                    wait(dve, m_in[prev.buf], (prev.round + 1) * 32)
                    nc.vector.tensor_copy(mrow[:, 0], psum[0:H, D0, 0:SQ]).then_inc(mhi_ready, 1)
                    dve.wait_ge(mhi_ready, bm.n + 1)
                    nc.vector.tensor_tensor(mrow[:, 1], psum[0:H, D0, 0:SQ], mrow[:, 0], ALU.subtract).then_inc(mrow_ready, 1)

            def route(g, p):
                n = tiles_of(g)
                done = [g * ROUTER_OPS]

                def link(ins):
                    done[0] = done[0] + 1
                    ins.then_inc(router, 1)
                    dve.wait_ge(router, done[0])

                esig, den, score, sfc = (rt[:, i, 0:n] for i in (0, 1, 2, 3))
                hi, lo, m1, m2 = (rt[:, i, 0:n, 0:4] for i in (4, 5, 6, 7))
                keep, masked, rank, w = (rt[:, i, 0:n] for i in (8, 9, 10, 11))
                halves = lambda v: v.rearrange("p t (g e) -> p t g e", g=2)
                dve.wait_ge(esig_ready, g + 1)
                link(nc.vector.tensor_scalar(den, esig, 1.0, None, ALU.add))
                link(nc.vector.reciprocal(score, den))
                link(nc.vector.tensor_tensor(sfc, score, gb_s[:].unsqueeze(1).broadcast_to([128, n, NE]), ALU.add))
                pair = sfc.rearrange("p t (q r) -> p t q r", r=2)
                link(nc.vector.tensor_tensor(hi, pair[:, :, :, 0], pair[:, :, :, 1], ALU.max))
                link(nc.vector.tensor_tensor(lo, pair[:, :, :, 0], pair[:, :, :, 1], ALU.min))
                two = lambda v: v.rearrange("p t (g r) -> p t g r", r=2)
                link(nc.vector.tensor_tensor(m1[:, :, 0:2], two(hi)[:, :, :, 0], two(hi)[:, :, :, 1], ALU.max))
                link(nc.vector.tensor_tensor(m1[:, :, 2:4], two(hi)[:, :, :, 0], two(hi)[:, :, :, 1], ALU.min))
                link(nc.vector.tensor_tensor(m2[:, :, 0:2], two(lo)[:, :, :, 0], two(lo)[:, :, :, 1], ALU.max))
                link(nc.vector.tensor_tensor(m2[:, :, 2:4], m1[:, :, 2:4], m2[:, :, 0:2], ALU.max))
                link(nc.vector.tensor_tensor(hi[:, :, 0:2], m1[:, :, 0:2], m2[:, :, 2:4], ALU.add))
                link(nc.vector.tensor_tensor(keep[:, :, 4:8], hi[:, :, 1:2].broadcast_to([128, n, 4]),
                                             hi[:, :, 0:1].broadcast_to([128, n, 4]), ALU.is_gt))
                link(nc.vector.tensor_scalar(keep[:, :, 0:4], keep[:, :, 4:8], -1.0, 1.0, ALU.mult, ALU.add))
                link(nc.vector.tensor_tensor(masked, sfc, keep, ALU.mult))
                mine = masked.unsqueeze(3).broadcast_to([128, n, NE, NE])
                other = masked.unsqueeze(2).broadcast_to([128, n, NE, NE])
                ge, gt = big[:, 0, 0:n], big[:, 1, 0:n]
                tie = lower[:].unsqueeze(1).broadcast_to([128, n, NE, NE])
                for t in range(n):
                    ins = nc.vector.tensor_tensor(ge[:, t], other[:, t], mine[:, t], ALU.is_equal)
                    ins2 = nc.vector.tensor_tensor(gt[:, t], other[:, t], mine[:, t], ALU.is_gt)
                link(ins2)
                link(nc.vector.tensor_tensor(ge, ge, tie, ALU.mult))
                link(nc.vector.tensor_tensor(gt, gt, ge, ALU.add))
                link(nc.vector.tensor_reduce(rank, gt, axis=AX_X, op=ALU.add))
                link(nc.vector.scalar_tensor_tensor(out=w, in0=rank, scalar=1.5, in1=score, op0=ALU.is_lt, op1=ALU.mult))
                link(nc.vector.tensor_reduce(den[:, :, 0:1], w, axis=AX_X, op=ALU.add))
                assert ROUTER_OPS == 19
                return w, den

            def ln(g, p, k, part):
                n = tiles_of(g)
                if part == "norm":
                    dve.wait_ge(ln_in[p], k * 16 + 16)
                    for t in range(n):
                        nc.vector.bn_stats(stats2[:, p, t], xin2[p][:, t]).then_inc(t_stats, 1)
                    aggregate(stats2[:, p, n - 1, 0:1], [(meanvar2[:, p, t], stats2[:, p, t]) for t in range(n)], 128,
                              t_stats, first_of(g) + n).then_inc(t_meanvar, 1)
                if part == "normalise":
                    dve.wait_ge(t_rstd, g + 1)
                    wait(dve, t_xnt_mm, first_of(g))
                    for t in range(n):
                        nc.vector.tensor_scalar(xn2[:, t], xin2[p][:, t], meanvar2[:, p, t, 0:1], rstd2[:, p, t:t + 1],
                                                ALU.subtract, ALU.mult).then_inc(t_xn, 1)
                if part != "route":
                    return
                w, den = route(g, p)
                nc.vector.tensor_scalar(rt[:, 4, 0:n, 0:1], den[:, :, 0:1], 1e-20, None, ALU.add).then_inc(norm_chain, 1)
                dve.wait_ge(norm_chain, 3 * g + 1)
                nc.vector.reciprocal(rt[:, 5, 0:n, 0:1], rt[:, 4, 0:n, 0:1]).then_inc(norm_chain, 1)
                dve.wait_ge(norm_chain, 3 * g + 2)
                nc.vector.tensor_scalar(rt[:, 6, 0:n, 0:1], rt[:, 5, 0:n, 0:1], g_tanh[:, 1:2], None,
                                        ALU.mult).then_inc(norm_chain, 1)
                dve.wait_ge(norm_chain, 3 * g + 3)
                wait(dve, acc_ready, SETS * (g - 1))
                nc.vector.scalar_tensor_tensor(out=cw[:, p, 0:n], in0=w, scalar=ROUTED_SCALE,
                                               in1=rt[:, 6, 0:n, 0:1].broadcast_to([128, n, NE]),
                                               op0=ALU.mult, op1=ALU.mult).then_inc(cw_ready, 1)

            def weights_lo_part(n):
                if n == 0:
                    dve.wait_ge(score_mm, UNITS * (B - 1))
                dve.wait_ge(weights_hi, n + 1)
                (w, hi, lo), at = WEIGHTS[n // 4], slice(n % 4 * PART, (n % 4 + 1) * PART)
                nc.vector.tensor_tensor(lo[:, at], w[:, at], hi[:, at], ALU.subtract).then_inc(lo_weights, 1)

            def accumulate(g, p, k, i):
                n = tiles_of(g)
                dve.wait_ge(down_mm, g * NJ + SHARED // HID + i)
                if i == 0:
                    wait(dve, y_out[p], k * 16)
                else:
                    wait(dve, acc_ready, g * SETS + i)
                bank = DOWN_BANK[(p + i) % 2]
                if i == 0:
                    for t in range(0, n, 2):
                        m = min(2, n - t)
                        ins = nc.vector.scalar_tensor_tensor(
                            out=y[:, p, t:t + m].rearrange("p t e -> p (t e)"), in0=psum[:, bank + t // 2, 0:m * E],
                            scalar=g_tanh[:, 1:2], in1=xin2[p][:, t:t + m].rearrange("p t e -> p (t e)"),
                            op0=ALU.mult, op1=ALU.add)
                else:
                    if i == 1:
                        dve.wait_ge(cw_ready, g + 1)
                    for t in range(n):
                        ins = nc.vector.scalar_tensor_tensor(
                            out=y[:, p, t], in0=psum[:, bank + t // 2, (t % 2) * E:(t % 2 + 1) * E],
                            scalar=cw[:, p, t, i - 1:i], in1=y[:, p, t], op0=ALU.mult, op1=ALU.add)
                ins.then_inc(acc_ready, 1)

            def ffn(now, ahead):
                for j in range(NJ):
                    if j == 0 and not (static(now[0]) and now[0] == 0):
                        ln(*now, "route")
                    if j >= SHARED // HID:
                        accumulate(*now, j - SHARED // HID)
                    if ahead and j == LN_STATS:
                        ln(*ahead, "norm")
                    if ahead and j == LN_NORM:
                        ln(*ahead, "normalise")
                accumulate(*now, SETS - 1)

            dve.wait_ge(ctx_hi_ready, 1)
            nc.vector.tensor_tensor(ctx_lo[:, 0, :, 0:SK], ctx_raw[:], ctx_hi[:, 0, :, 0:SK], ALU.subtract).then_inc(ctx_ready, 1)
            dve.wait_ge(wkv_hi_ready, 1)
            nc.vector.tensor_tensor(wk_lo[:], wk_raw, wk_hi[:], ALU.subtract).then_inc(wkv_lo_ready, 1)

            def split_wv():
                dve.wait_ge(wkv_hi_ready, 2)
                nc.vector.tensor_tensor(wv_lo[:], wv_raw, wv_hi[:], ALU.subtract).then_inc(wkv_lo_ready, 1)

            phase1(dve, step, {-2: split_wv, -1: fill_v_and_bias})
            phase2(dve, ffn)

        @block.tensor
        def _(pe):
            mm = nc.tensor.matmul
            pe.wait_ge(weights_in, N_WEIGHTS)
            pe.wait_ge(made, 4)

            def row_scores(b, h):
                wait(pe, max_ready, H * b.n + h - 1)
                if h == 0:
                    pe.wait_ge(qs_in[b.buf], (b.round + 1) * (6 * 16))
                    pe.wait_ge(ks_in[b.buf], (b.round + 1) * (3 * 16))
                mm(psum[0:SQ, ROW_BANK[h % 2], 0:SK], qs[0:ROWS, b.buf, h], ks[b.buf][0:ROWS, h],
                   start=True, stop=True).then_inc(row_mm, 1)

            def k_proj(b, half):
                if half == 0:
                    pe.wait_ge(ctx_ready, b.n + 1)
                    wait(pe, mrow_ready, upto(1, b.n - 2))
                    if static(b.n) and b.n <= 2:
                        wait(pe, k_ready, 2 * b.n - 1)
                else:
                    wait(pe, v_ready, upto(NT, b.n - 2, 2))
                    if static(b.n) and b.n <= 1:
                        wait(pe, k_ready, 2 * b.n)
                at = slice(half * 128, (half + 1) * 128)
                parts = [(w[:, c, at], v[:, b.buf, c]) for c in range(CI)
                         for w, v in ((wk_hi, ctx_hi), (wk_hi, ctx_lo), (wk_lo, ctx_hi))]
                for i, (w, v) in enumerate(parts):
                    ins = mm(psum[:, (D0, D1)[half], 0:SKP], w, v, start=(i == 0), stop=(i == len(parts) - 1))
                ins.then_inc(k_mm, 1)

            def x_transpose(b):
                pe.wait_ge(xn_ready, b.n + 1)
                wait(pe, att0_ready, b.n - 3)
                if static(b.n) and b.n <= 3:
                    wait(pe, v_ready, NT * (b.n - 1))
                    wait(pe, q_ready, b.n)
                for c in range(CI):
                    ins = nc.tensor.transpose(psum[:, D2, c * SQ:(c + 1) * SQ], xn[:, c * 128:(c + 1) * 128], ident[0:SQ, 0:SQ])
                ins.then_inc(xnt_mm, 1)

            def q_proj(b):
                pe.wait_ge(xnt_ready, b.n + 1)
                for half in range(2):
                    for c in range(CI):
                        ins = mm(psum[:, D2, half * SQ:(half + 1) * SQ], wq_s[:, c, half * 128:(half + 1) * 128],
                                 xnt[:, c], start=(c == 0), stop=(c == CI - 1))
                ins.then_inc(q_mm, 1)

            def v_proj(b, t):
                if t == 0:
                    wait(pe, q_ready, upto(1, b.n + 2))
                    if static(b.n) and b.n + 1 >= B:
                        pe.wait_ge(att0_ready, b.n - 2)
                elif t == 1:
                    wait(pe, x2_ready, b.n - 2)
                    if static(b.n) and b.n <= 2:
                        pe.wait_ge(k_ready, 2 * b.n + 4)
                else:
                    pe.wait_ge(v_ready, NT * b.n + 1)
                parts = [(v[:, b.buf, c, t * KSTEP:t * KSTEP + KT], w[:, c]) for c in range(CI)
                         for v, w in ((ctx_hi, wv_hi), (ctx_hi, wv_lo), (ctx_lo, wv_hi))]
                for i, (v, w) in enumerate(parts):
                    ins = mm(psum[0:KT, (D2, D1, D2)[t], 0:E], v, w, start=(i == 0), stop=(i == len(parts) - 1))
                ins.then_inc(v_mm, 1)

            def scores(b, u):
                wait(pe, exp_ready, UNITS * b.n + u - 1)
                if u == 0:
                    pe.wait_ge(m_in[b.buf], (b.round + 1) * 32)
                c, t = unit(u)
                for j in range(HPU):
                    h = c * HPU + j
                    ins = mm(psum[0:KT, SCORE_BANK[u % 2], j * SQ:(j + 1) * SQ], ks[b.buf][0:MROWS, h, t * KSTEP:t * KSTEP + KT],
                             qs[0:MROWS, b.buf, h], start=True, stop=True)
                ins.then_inc(score_mm, 1)

            def times_v(b, u):
                pe.wait_ge(exp_ready, UNITS * b.n + u + 1)
                if u == 0:
                    pe.wait_ge(v_ready, NT * (b.n + 1))
                    wait(pe, pvt_ready, b.n)
                c, t = unit(u)
                n = KT if t == NT - 1 else KSTEP
                for j in range(HPU):
                    ins = mm(psum[j * DV:(j + 1) * DV, PV_BANK, c * SQ:(c + 1) * SQ], vs[0:n, b.buf, t, c * HPU + j],
                             probs[0:n, u, j * SQ:(j + 1) * SQ], start=(t == 0), stop=(t == NT - 1))
                ins.then_inc(pv_mm, 1)

            def pv_transpose(b):
                pe.wait_ge(pvt_ready, b.n + 1)
                wait(pe, v_ready, upto(NT, b.n + 3))
                if static(b.n) and b.n + 2 >= B:
                    pe.wait_ge(att0_ready, b.n)
                for c in range(H // HPU):
                    ins = nc.tensor.transpose(psum[0:SQ, D2, c * 128:(c + 1) * 128], pvt[:, c * SQ:(c + 1) * SQ], ident[:])
                ins.then_inc(pvt_mm, 1)

            def att_transpose(b):
                pe.wait_ge(att_ready, b.n + 1)
                wait(pe, k_ready, upto(2, b.n + 4, 1))
                if static(b.n) and b.n + 4 >= B:
                    pe.wait_ge(mrow_ready, upto(1, b.n + 2))
                for c in range(CI):
                    ins = nc.tensor.transpose(psum[:, D0, c * SQ:(c + 1) * SQ], att[:, c * 128:(c + 1) * 128], ident[0:SQ, 0:SQ])
                ins.then_inc(att_t_mm, 1)

            def out_proj(b):
                pe.wait_ge(att_t_ready, b.n + 1)
                wait(pe, k_ready, upto(2, b.n + 4, 2))
                if static(b.n) and b.n + 4 >= B:
                    pe.wait_ge(v_ready, upto(NT, b.n + 2, 2))
                for c in range(CI):
                    ins = mm(psum[0:SQ, D1, 0:E], att_t[:, c], wo_s[:, c], start=(c == 0), stop=(c == CI - 1))
                ins.then_inc(o_mm, 1)

            def max_transpose(b):
                pe.wait_ge(max_ready, H * (b.n + 1))
                wait(pe, att_t_ready, b.n - 1)
                if static(b.n) and (b.n <= 1 or b.n + 2 >= B):
                    pe.wait_ge(k_ready, upto(2, b.n + 2, 1))
                nc.tensor.transpose(psum[0:H, D0, 0:SQ], negmax[:], ident[0:SQ, 0:SQ]).then_inc(mt_mm, 1)

            def step(bl, bv, bm, be, bf):
                for i in range(H):
                    if not (bl or bv or bm or be) and i in FIRST_SLOTS:
                        slot((0, 0, 0), (1, 1, 0), FIRST_SLOTS[i])
                    if bm is not None and i == 0:
                        row_scores(bm, 0)
                    if bf is not None and i == SUM_AT:
                        pv_transpose(bf)
                    if be is not None and 2 <= i < 2 + UNITS:
                        scores(be, i - 2)
                    if bl is not None and i in K_AT:
                        k_proj(bl, K_AT.index(i))
                    if bm is not None and i + 1 < H:
                        row_scores(bm, i + 1)
                    if bl is not None and i == X_AT:
                        x_transpose(bl)
                    if bf is not None and i == ATT_AT:
                        att_transpose(bf)
                    if bl is not None and i == Q_AT:
                        q_proj(bl)
                    if bf is not None and i == OUT_AT:
                        out_proj(bf)
                    if be is not None and 4 <= i < 4 + UNITS:
                        times_v(be, i - 4)
                    if be is not None and at_end(be) and i == FIRST_LN_AT:
                        transposes_first()
                if bm is not None:
                    max_transpose(bm)
                if bv is not None:
                    for t in range(NT):
                        v_proj(bv, t)

            def ln(g, p, k, part):
                n = tiles_of(g)
                if part in range(n):
                    t = part
                    pe.wait_ge(t_xn, first_of(g) + t + 1)
                    wait(pe, t_xhi, first_of(g) + t)
                    for c in range(CI):
                        ins = nc.tensor.transpose(psum[:, LN_BANK, c * 128:(c + 1) * 128],
                                                  xn2[:, t, c * 128:(c + 1) * 128], ident[:])
                    ins.then_inc(t_xnt_mm, 1)
                if part != "route":
                    return
                pe.wait_ge(t_xhi, first_of(g) + n)
                wait(pe, esig_ready, g)
                for t in range(n):
                    for c in range(CI):
                        ins = mm(psum[:, LOGIT_BANK, t * NE:(t + 1) * NE], xraw[:, c, t * 128:(t + 1) * 128], gate_s[:, c],
                                 start=(c == 0), stop=(c == CI - 1))
                ins.then_inc(logit_mm, 1)

            def up(g, p, k, j):
                if j == 0:
                    pe.wait_ge(t_xlo, first_of(g) + tiles_of(g))
                wait(pe, relu_ready, g * NJ + j - 1)
                n = tiles_of(g) * 128
                at = slice(j * HID, (j + 1) * HID)
                parts = [(w[:, c, at], v[p][:, c, 0:n]) for c in range(CI)
                         for w, v in ((up_hi, xhi), (up_hi, xlo), (up_lo, xhi))]
                for i, (w, v) in enumerate(parts):
                    ins = mm(psum[:, UP_BANK[j % 2], 0:n], w, v, start=(i == 0), stop=(i == len(parts) - 1))
                ins.then_inc(up_mm, 1)

            def down(g, p, k, j):
                pe.wait_ge(lo_ready, g * NJ + j + 1)
                i = max(0, j - SHARED // HID + 1)
                first = j == 0 or i > 0
                if first:
                    wait(pe, acc_ready, g * SETS + i - 1)
                for t in range(tiles_of(g)):
                    at = slice(t * 128, (t + 1) * 128)
                    parts = ((sq_hi, down_hi), (sq_hi, down_lo), (sq_lo, down_hi))
                    for q, (v, w) in enumerate(parts):
                        ins = mm(psum[:, DOWN_BANK[(p + i) % 2] + t // 2, (t % 2) * E:(t % 2 + 1) * E], v[:, j % 3, at], w[:, j],
                                 start=(first and t % 2 == 0 and q == 0),
                                 stop=((i > 0 or j == SHARED // HID - 1) and q == 2), skip_group_check=True)
                ins.then_inc(down_mm, 1)

            def slot(now, ahead, j):
                if j + 2 < NJ:
                    up(*now, j + 2)
                elif ahead:
                    up(*ahead, j + 2 - NJ)
                down(*now, j)
                if ahead and 0 <= j - LN_T < GT:
                    ln(*ahead, j - LN_T)
                if ahead and j == LN_T + GT:
                    ln(*ahead, "route")

            def ffn(now, ahead):
                if isinstance(now[0], int) and now[0] == 0:
                    pe.wait_ge(x2_ready, B)
                    pe.wait_ge(att0_ready, B)
                    pe.wait_ge(mrow_ready, B)
                for j in slots_left(now[0]):
                    slot(now, ahead, j)

            def transposes_first():
                pe.wait_ge(max_ready, H * B)
                for t in range(tiles_of(0)):
                    ln(0, 0, 0, t)

            def ups_first():
                ln(0, 0, 0, "route")
                pe.wait_ge(exp_ready, UNITS * B)
                pe.wait_ge(lo_weights, 8)
                for j in range(2):
                    up(0, 0, 0, j)

            phase1(pe, step, {-3: lambda: (pe.wait_ge(fills, 1), pe.wait_ge(wkv_lo_ready, 1)),
                              -2: lambda: (pe.wait_ge(consts, N_CONST), pe.wait_ge(wkv_lo_ready, 2)),
                              0: lambda: (pe.wait_ge(fills, 2), pe.wait_ge(made, 5), pe.wait_ge(ones_in, 32)),
                              B: ups_first})
            phase2(pe, ffn)


_ORDER = ("x", "ctx_t", "g_x", "g_f", "wq", "bq", "wk", "bk", "wv", "bv", "wo", "bo",
          "gate_t", "gate_b", "up_t", "down_t", "sup_t", "sdown_t")


def kernel(**inputs):
    import numpy as np
    import concourse.bacc as bacc
    from concourse.bass_utils import run_bass_kernel_spmd as run

    i = {k: np.asarray(v) for k, v in inputs.items()}

    def by_dim(w):
        return w.reshape(w.shape[:-1] + (H, D)).swapaxes(-1, -2).reshape(w.shape)

    laid = {
        "x": i["x"].reshape(TOK, E),
        "ctx_t": i["ctx_1024"].transpose(0, 2, 1),
        "g_x": i["g_xattn"], "g_f": i["g_ffn"],
        "wq": by_dim(i["L0_xattn_Wq"]), "bq": by_dim(i["L0_xattn_bq"]),
        "wk": by_dim(i["L0_xattn_Wk"]), "bk": by_dim(i["L0_xattn_bk"]),
        "wv": i["L0_xattn_Wv"], "bv": i["L0_xattn_bv"], "wo": i["L0_xattn_Wo"], "bo": i["L0_xattn_bo"],
        "gate_t": i["L0_ffn_gate_weight"].T, "gate_b": i["L0_ffn_gate_bias"],
        "up_t": i["L0_ffn_up_weights"].reshape(NE * HID, E).T,
        "down_t": i["L0_ffn_down_weights"].transpose(0, 2, 1).reshape(NE * HID, E),
        "sup_t": i["L0_ffn_shared_up_weight"].T, "sdown_t": i["L0_ffn_shared_down_weight"].T,
    }
    nc = bacc.Bacc("TRN2", target_bir_lowering=False, num_devices=1)
    arrays, args = {}, []
    for name in _ORDER:
        a = np.ascontiguousarray(laid[name])
        arrays[f"in_{name}"] = a
        args.append(nc.dram_tensor(f"in_{name}", a.shape, mybir.dt.from_np(a.dtype), kind="ExternalInput").ap())
    args.append(nc.dram_tensor("out_0", (TOK, E), F32, kind="ExternalOutput").ap())
    build(nc, *args)
    r = run(nc, [arrays], core_ids=[0])
    return r.results[0]["out_0"].reshape(B, SQ, E)
```
